# Optimizing a Trainium2 kernel written in Bass

```python
import numpy as np
import jax
import jax.numpy as jnp

def _softmax(x, axis=-1):
    return jax.nn.softmax(x, axis=axis)

def _gelu(x):
    return jax.nn.gelu(x, approximate=True)

def _silu(x):
    return jax.nn.silu(x)

def _sigmoid(x):
    return jax.nn.sigmoid(x)

def _layernorm(x, axis=-1, eps=1e-05):
    m = jnp.mean(x, axis=axis, keepdims=True)
    v = jnp.var(x, axis=axis, keepdims=True)
    return (x - m) / jnp.sqrt(v + eps)

def _scatter_add(tgt, idx, src, axis=0):
    return tgt.at[idx].add(src)

def _segment_sum(src, seg, n):
    return jax.ops.segment_sum(src, seg, n)
kernel_name = 'mk_adj_preln_d4_adj_r2_9ab509'

def setup_inputs(seed: int=0):
    np.random.seed(seed)
    _w = jnp.asarray

    def _rec_inputs():
        import jax
        import jax.numpy as jnp
        _gk = jax.random.key(seed)
        x = 7.22e-05 + 1 * jax.random.normal(jax.random.fold_in(_gk, 1), (128, 128, 256), jnp.float32)
        _a = jax.random.bernoulli(jax.random.fold_in(_gk, 2), 0.125, (128, 128, 128))
        _a = jnp.logical_or(_a, jnp.swapaxes(_a, -1, -2))
        _a = jnp.logical_or(_a, jnp.eye(128, dtype=bool))
        _af = _a.astype(jnp.float32)
        _af = _af * jax.random.uniform(jax.random.fold_in(_gk, 3), (128, 128, 128), jnp.float32, 0.05, 1)
        adj = _af
        return (x, adj)
    x, adj = _rec_inputs()

    def _L0_gnn_setup():
        import jax, jax.numpy as jnp
        import numpy as np
        EPS_LN = 1e-05

        def hypergraph_conv(x, adj, W, b):
            N, C, _ = adj.shape
            H = (adj != 0).astype(x.dtype)
            w = adj.reshape(N, -1)[:, :C]
            xw = jnp.einsum('ncd,hd->nch', x, W)
            Dn = jnp.einsum('nce,ne->nc', H, w)
            Dn = jnp.where(Dn > 0, 1.0 / Dn, 0.0)
            Be = H.sum(axis=1)
            Be = jnp.where(Be > 0, 1.0 / Be, 0.0)
            m = Be[:, :, None] * jnp.einsum('nce,nch->neh', H, xw)
            out = Dn[:, :, None] * jnp.einsum('nce,neh->nch', H, m)
            return out + b

        def layer_norm(x, g, b):
            mu = jnp.mean(x, axis=-1, keepdims=True)
            var = jnp.var(x, axis=-1, keepdims=True)
            return (x - mu) * jax.lax.rsqrt(var + EPS_LN) * g + b
        key = jax.random.key(seed)
        ks = jax.random.split(key, 4)
        N, C, Din, Dh, Dout = (16, 512, 256, 512, 256)
        x = jax.random.normal(ks[0], (N, C, Din), dtype=jnp.float32)
        adj = jax.random.uniform(ks[1], (N, C, C), dtype=jnp.float32, minval=0.1, maxval=1.0)
        W1 = jax.random.normal(ks[2], (Dh, Din), dtype=jnp.float32) * (1.0 / np.sqrt(Din))
        b1 = jnp.zeros((Dh,), dtype=jnp.float32)
        gamma = jnp.ones((Dh,), dtype=jnp.float32)
        beta = jnp.zeros((Dh,), dtype=jnp.float32)
        W2 = jax.random.normal(ks[3], (Dout, Dh), dtype=jnp.float32) * (1.0 / np.sqrt(Dh))
        b2 = jnp.zeros((Dout,), dtype=jnp.float32)
        return {'x': x, 'adj': adj, 'W1': W1, 'b1': b1, 'gamma': gamma, 'beta': beta, 'W2': W2, 'b2': b2}
    _L0_gnn_all = _L0_gnn_setup()
    _L0_gnn_in = {k: v for k, v in _L0_gnn_all.items() if k in ('W1', 'b1', 'gamma', 'beta', 'W2', 'b2')}
    del _L0_gnn_all

    def _L1_gnn_setup():
        import jax, jax.numpy as jnp
        import numpy as np
        B, N, DIN, DOUT = (8, 1024, 256, 256)
        EDGE_P = 0.01

        def _gcn_norm(adj):
            A = (adj != 0).astype(adj.dtype)
            eye = jnp.eye(A.shape[-1], dtype=A.dtype)
            A = jnp.maximum(A, eye)
            deg = A.sum(axis=-1)
            dinv = jnp.where(deg > 0, jax.lax.rsqrt(deg), 0.0)
            return dinv[..., :, None] * A * dinv[..., None, :]
        key = jax.random.key(seed)
        k1, k2, k3, k4 = jax.random.split(key, 4)
        inputs = jax.random.normal(k1, (B, N, DIN), dtype=jnp.float32)
        adj = (jax.random.uniform(k2, (B, N, N)) < EDGE_P).astype(jnp.float32)
        W = jax.random.normal(k3, (DIN, DOUT), dtype=jnp.float32) / np.sqrt(DIN)
        b = jax.random.normal(k4, (DOUT,), dtype=jnp.float32) * 0.01
        return {'inputs': inputs, 'adj': adj, 'W': W, 'b': b}
    _L1_gnn_all = _L1_gnn_setup()
    _L1_gnn_in = {k: v for k, v in _L1_gnn_all.items() if k in ('W', 'b')}
    del _L1_gnn_all

    def _L2_gnn_setup():
        import jax, jax.numpy as jnp
        import numpy as np
        B, N, D_IN, D_OUT = (4, 2048, 256, 256)
        key = jax.random.key(seed)
        k1, k2, k3, k4 = jax.random.split(key, 4)
        x = jax.random.normal(k1, (B, N, D_IN), dtype=jnp.float32)
        A_shape = jax.random.uniform(k2, (B, N, N), dtype=jnp.float32)
        w = jax.random.normal(k3, (D_IN, D_OUT), dtype=jnp.float32)
        a = jax.random.normal(k4, (D_OUT,), dtype=jnp.float32)
        return {'x': x, 'A_shape': A_shape, 'w': w, 'a': a}
    _L2_gnn_all = _L2_gnn_setup()
    _L2_gnn_in = {k: v for k, v in _L2_gnn_all.items() if k in ('w', 'a')}
    del _L2_gnn_all

    def _L3_gnn_setup():
        import jax, jax.numpy as jnp
        import numpy as np
        B, N, F_IN, F_HID, F_OUT = (32, 512, 256, 256, 256)

        def _gcn_layer(x, adj, W, b):
            support = jnp.einsum('bnf,fh->bnh', x, W)
            return jnp.einsum('bnm,bmh->bnh', adj, support) + b
        key = jax.random.key(seed)
        ks = jax.random.split(key, 8)

        def xavier(k, fan_in, fan_out):
            bound = float(np.sqrt(6.0 / (fan_in + fan_out)))
            return jax.random.uniform(k, (fan_in, fan_out), jnp.float32, -bound, bound)
        return {'batch_graph': jax.random.normal(ks[0], (B, N, F_IN), jnp.float32), 'adj': jax.random.uniform(ks[1], (B, N, N), jnp.float32), 'W1': xavier(ks[2], F_IN, F_HID), 'b1': jnp.zeros((F_HID,), jnp.float32), 'W2': xavier(ks[3], F_HID, F_HID), 'b2': jnp.zeros((F_HID,), jnp.float32), 'W3': xavier(ks[4], F_HID, F_OUT), 'b3': jnp.zeros((F_OUT,), jnp.float32)}
    _L3_gnn_all = _L3_gnn_setup()
    _L3_gnn_in = {k: v for k, v in _L3_gnn_all.items() if k in ('W1', 'b1', 'W2', 'b2', 'W3', 'b3')}
    del _L3_gnn_all
    return {'x': x, 'adj': adj, 'L0_gnn_W1': _L0_gnn_in['W1'], 'L0_gnn_b1': _L0_gnn_in['b1'], 'L0_gnn_gamma': _L0_gnn_in['gamma'], 'L0_gnn_beta': _L0_gnn_in['beta'], 'L0_gnn_W2': _L0_gnn_in['W2'], 'L0_gnn_b2': _L0_gnn_in['b2'], 'L1_gnn_W': _L1_gnn_in['W'], 'L1_gnn_b': _L1_gnn_in['b'], 'L2_gnn_w': _L2_gnn_in['w'], 'L2_gnn_a': _L2_gnn_in['a'], 'L3_gnn_W1': _L3_gnn_in['W1'], 'L3_gnn_b1': _L3_gnn_in['b1'], 'L3_gnn_W2': _L3_gnn_in['W2'], 'L3_gnn_b2': _L3_gnn_in['b2'], 'L3_gnn_W3': _L3_gnn_in['W3'], 'L3_gnn_b3': _L3_gnn_in['b3']}

def reference(x, adj, L0_gnn_W1, L0_gnn_b1, L0_gnn_gamma, L0_gnn_beta, L0_gnn_W2, L0_gnn_b2, L1_gnn_W, L1_gnn_b, L2_gnn_w, L2_gnn_a, L3_gnn_W1, L3_gnn_b1, L3_gnn_W2, L3_gnn_b2, L3_gnn_W3, L3_gnn_b3):
    import jax
    import jax.numpy as jnp

    def _L0_gnn_ref(x, adj, W1, b1, gamma, beta, W2, b2):
        import jax, jax.numpy as jnp
        import numpy as np
        EPS_LN = 1e-05

        def hypergraph_conv(x, adj, W, b):
            N, C, _ = adj.shape
            H = (adj != 0).astype(x.dtype)
            w = adj.reshape(N, -1)[:, :C]
            xw = jnp.einsum('ncd,hd->nch', x, W)
            Dn = jnp.einsum('nce,ne->nc', H, w)
            Dn = jnp.where(Dn > 0, 1.0 / Dn, 0.0)
            Be = H.sum(axis=1)
            Be = jnp.where(Be > 0, 1.0 / Be, 0.0)
            m = Be[:, :, None] * jnp.einsum('nce,nch->neh', H, xw)
            out = Dn[:, :, None] * jnp.einsum('nce,neh->nch', H, m)
            return out + b

        def layer_norm(x, g, b):
            mu = jnp.mean(x, axis=-1, keepdims=True)
            var = jnp.var(x, axis=-1, keepdims=True)
            return (x - mu) * jax.lax.rsqrt(var + EPS_LN) * g + b
        h = jax.nn.relu(hypergraph_conv(x, adj, W1, b1))
        h = layer_norm(h, gamma, beta)
        y = hypergraph_conv(h, adj, W2, b2)
        return y + x

    def _L1_gnn_ref(inputs, adj, W, b):
        import jax, jax.numpy as jnp
        import numpy as np
        B, N, DIN, DOUT = (8, 1024, 256, 256)
        EDGE_P = 0.01

        def _gcn_norm(adj):
            A = (adj != 0).astype(adj.dtype)
            eye = jnp.eye(A.shape[-1], dtype=A.dtype)
            A = jnp.maximum(A, eye)
            deg = A.sum(axis=-1)
            dinv = jnp.where(deg > 0, jax.lax.rsqrt(deg), 0.0)
            return dinv[..., :, None] * A * dinv[..., None, :]
        norm = _gcn_norm(adj)
        h = jnp.einsum('bnf,fo->bno', inputs, W)
        agg = jnp.einsum('bnm,bmo->bno', norm, h)
        return jnp.tanh(agg + b)

    def _L2_gnn_ref(x, A_shape, w, a):
        import jax, jax.numpy as jnp
        import numpy as np
        B, N, D_IN, D_OUT = (4, 2048, 256, 256)
        y = x @ w
        s = y @ a
        A = s[..., :, None] + s[..., None, :]
        A = jnp.tanh(A / 8.0) * 8.0
        A = jnp.where(A >= 0, A, 0.1 * A)
        A = jnp.exp(A) * A_shape
        A = A / jnp.sum(A, axis=-1, keepdims=True)
        A = A * jnp.sum(A_shape, axis=-1, keepdims=True)
        out = A @ x @ w
        return out

    def _L3_gnn_ref(batch_graph, adj, W1, b1, W2, b2, W3, b3):
        import jax, jax.numpy as jnp
        import numpy as np
        B, N, F_IN, F_HID, F_OUT = (32, 512, 256, 256, 256)

        def _gcn_layer(x, adj, W, b):
            support = jnp.einsum('bnf,fh->bnh', x, W)
            return jnp.einsum('bnm,bmh->bnh', adj, support) + b
        x = jax.nn.relu(_gcn_layer(batch_graph, adj, W1, b1))
        x = jax.nn.relu(_gcn_layer(x, adj, W2, b2))
        out = _gcn_layer(x, adj, W3, b3)
        return out
    h = jnp.maximum(_layernorm(x, axis=-1), 0.0)
    x = x + _L0_gnn_ref(h, adj, L0_gnn_W1, L0_gnn_b1, L0_gnn_gamma, L0_gnn_beta, L0_gnn_W2, L0_gnn_b2)
    h = jnp.maximum(_layernorm(x, axis=-1), 0.0)
    x = x + _L1_gnn_ref(h, adj, L1_gnn_W, L1_gnn_b)
    h = jnp.maximum(_layernorm(x, axis=-1), 0.0)
    x = x + _L2_gnn_ref(h, adj, L2_gnn_w, L2_gnn_a)
    h = jnp.maximum(_layernorm(x, axis=-1), 0.0)
    x = x + _L3_gnn_ref(h, adj, L3_gnn_W1, L3_gnn_b1, L3_gnn_W2, L3_gnn_b2, L3_gnn_W3, L3_gnn_b3)
    return x

_drawn_inputs = setup_inputs


def setup_inputs(seed=0):
    import zlib

    import numpy as np

    out = dict(_drawn_inputs(seed))
    spreads = {'L0_gnn_b1': (0.0, 0.1),
     'L0_gnn_gamma': (1.0, 0.2),
     'L0_gnn_beta': (0.0, 0.1),
     'L0_gnn_b2': (0.0, 0.607),
     'L3_gnn_b1': (0.0, 0.8),
     'L3_gnn_b2': (0.0, 2.0),
     'L3_gnn_b3': (0.0, 2.0)}
    factors = {'L1_gnn_b': 63.917}
    for name, (base, spread) in spreads.items():
        noise = np.random.default_rng([zlib.crc32(name.encode()), seed]).standard_normal(out[name].shape)
        drawn = base * np.exp(spread * noise) if base else spread * noise
        out[name] = jnp.asarray(drawn.astype(out[name].dtype))
    for name, factor in factors.items():
        out[name] = (out[name] * factor).astype(out[name].dtype)
    return out
```

```python
from contextlib import ExitStack

import concourse.bass as bass
from concourse import mybir
from concourse.alu_op_type import AluOpType as ALU

F32 = mybir.dt.float32
ACT = mybir.ActivationFunctionType
P = 128
J = 4
LN_EPS = 1e-5
TINY = 1.1754944e-38

PE_ORDER = [
    ("B", "2U", -1), ("B", "2W", -1), ("A", "G", 0), ("A", "0U", 0), ("A", "0W", 0), ("B", "3S", -1),
    ("B", "3U", -1), ("B", "3W", -1), ("A", "1U", 0), ("B", "4U", -1), ("B", "4W", -1), ("A", "1W", 0),
    ("B", "5U", -1), ("B", "5W", -1), ("A", "2U", 0), ("A", "2W", 0), ("B", "6U", -1), ("B", "6W", -1),
    ("A", "3S", 0), ("A", "3U", 0), ("A", "3W", 0), ("B", "G", 0), ("B", "0U", 0), ("A", "4U", 0),
    ("A", "4W", 0), ("B", "0W", 0), ("A", "5U", 0), ("A", "5W", 0), ("B", "1U", 0), ("A", "6U", 0),
    ("A", "6W", 0), ("B", "1W", 0)]
ACT_ORDER = [
    ("B", "2U", -1), ("A", "P", 0), ("A", "G", 0), ("A", "0U", 0), ("B", "2W", -1), ("B", "3S", -1),
    ("B", "3U", -1), ("A", "1U", 0), ("B", "3W", -1), ("B", "4U", -1), ("B", "4W", -1),
    ("B", "5U", -1), ("A", "1W", 0), ("A", "2U", 0), ("B", "5W", -1), ("B", "6U", -1), ("A", "2W", 0),
    ("A", "3S", 0), ("A", "3U", 0), ("B", "P", 0), ("B", "G", 0), ("B", "0U", 0), ("A", "3W", 0), ("A", "4U", 0),
    ("A", "4W", 0), ("A", "5U", 0), ("B", "1U", 0), ("A", "5W", 0), ("A", "6U", 0), ("B", "1W", 0)]
DVE_ORDER = [
    ("A", "P", 0), ("B", "2W", -1), ("A", "0W", 0), ("B", "3S", -1), ("A", "0N", 0), ("B", "3W", -1),
    ("B", "4W", -1), ("A", "1W", 0), ("B", "5W", -1), ("A", "2W", 0), ("B", "6W", -1), ("A", "3S", 0),
    ("B", "P", 0), ("A", "3W", 0), ("A", "4W", 0), ("B", "0W", 0), ("B", "0N", 0), ("A", "5W", 0),
    ("A", "6W", 0), ("B", "1W", 0)]
POOL_ORDER = [
    ("A", "P", 0), ("B", "2W", -1), ("A", "R", 0), ("A", "0N", 0), ("B", "3W", -1),
    ("A", "1W", 0), ("A", "2W", 0), ("B", "P", 0), ("B", "R", 0), ("A", "3W", 0),
    ("B", "0N", 0), ("B", "1W", 0)]


def program(nc, xs, adj_t, adj_r, adj_w, w1t, w2t, l1w, l2w, l2wt, l3w1, l3w2, l3w3,
            cols, b1, b2, l1b, l3b1, l3b2, l3b3, out):
    GROUPS = xs.shape[0]
    D = l1w.shape[2]
    DC = D // P
    DH = w1t.shape[2]
    HC = DH // P
    STREAMS = ("A", "B")

    with ExitStack() as ctx:
        def sb(name, shape, dt=F32):
            return ctx.enter_context(nc.sbuf_tensor(name, shape, dt))

        sems = {}
        PER_STREAM = ("x_loaded", "t_loaded", "r_loaded", "w_loaded", "stored")

        def sem(name, s=""):
            key = f"{name}_{s}" if name in PER_STREAM else name
            if key not in sems:
                sems[key] = ctx.enter_context(nc.semaphore(key))
            return sems[key]

        W1 = sb("W1", [P, DC, DH])
        W2 = sb("W2", [P, HC, D])
        W2G = sb("W2G", [P, HC, D])
        L1W, L2W, L2WT, L3W1, L3W2, L3W3 = (sb(n, [P, DC, D]) for n in ("L1W", "L2W", "L2WT", "L3W1", "L3W2", "L3W3"))
        COLS = sb("COLS", [P, 2 * HC + DC])
        GAMMA, BETA, ACOL = COLS[:, 0:HC], COLS[:, HC:2 * HC], COLS[:, 2 * HC:]
        B1 = sb("B1", [P, DH])
        B2, L1B, L3B1, L3B2, L3B3 = (sb(n, [P, D]) for n in ("B2", "L1B", "L3B1", "L3B2", "L3B3"))
        BW = sb("BW", [P, D])
        WA = sb("WA", [P, D])
        SPREAD = sb("SPREAD", [P, HC + DC, P])
        IDENT = sb("IDENT", [P, P])
        ONES = sb("ONES", [P, P])
        OFFDIAG = sb("OFFDIAG", [P, P])
        MHALF = sb("MHALF", [P, J])
        EIGHTH = sb("EIGHTH", [P, J])

        def per_stream(name, *shape):
            return {s: sb(f"{name}_{s}", [P, *shape]) for s in STREAMS}

        X = per_stream("X", J, D)
        T = per_stream("T", J, P)
        R = per_stream("R", J, P)
        WR = per_stream("WR", J, P)
        HT = per_stream("HT", J, P)
        BHT = per_stream("BHT", J, P)
        AT = per_stream("AT", J, P)
        G = per_stream("G", J, P)
        JUNK = per_stream("JUNK", J, 3, P)
        H = per_stream("H", J, D)
        U = per_stream("U", J, DH)
        Z = per_stream("Z", J, DH)
        RES = per_stream("RES", J, D)
        TMP = per_stream("TMP", J, D)
        E = per_stream("E", J, P)
        AE = per_stream("AE", J, P)
        O = per_stream("O", J, D)
        BN = per_stream("BN", J, 6)
        LN = per_stream("LN", 7, J)
        SUM, DIF, M2, DSQ, VE, NMU, RSTD = range(7)
        NB = per_stream("NB", J)
        ST = per_stream("ST", 16, J)
        CNT, BE, DNS, DN, DNI, DGH, DGI, DG1, DINV, S2, RSR, RSA, RR, SC, S8, CNM = range(16)

        UB = [ctx.enter_context(nc.psum_tensor(f"UB{j}", [P, 512], F32)) for j in range(J)]
        WB = [ctx.enter_context(nc.psum_tensor(f"WB{j}", [P, 512], F32)) for j in range(J)]

        block = ctx.enter_context(nc.Block())

        def done_at(s, k, j):
            return 2 * J * k + J * STREAMS.index(s) + j + 1

        LIVE = (("A", 0), ("B", 0), ("A", -1), ("B", -1))

        def run(eng, order, parts):
            def values(k):
                return {(s, back): dict(v=[done_at(s, k + back, j) for j in range(J)], dma=16 * (k + back + 1))
                        for s, back in LIVE}

            for s, step, back in order:
                if not back:
                    parts[step](s, values(0)[s, 0], 0)
            with eng.Fori(1, GROUPS) as k:
                loop = {(s, back): dict(v=[eng.snap(2 * J * k + done_at(s, back, j)) for j in range(J)])
                        for s, back in LIVE}
                dma = {back: eng.snap(16 * k + 16 * (back + 1)) for back in (0, -1)}
                for s, back in LIVE:
                    loop[s, back]["dma"] = dma[back]
                for s, step, back in order:
                    parts[step](s, loop[s, back], loop)
            for s, step, back in order:
                if back:
                    parts[step](s, values(GROUPS)[s, back], GROUPS)

        @block.sync
        def _(sp):
            for dst, src in ((W1, w1t), (W2, w2t), (L2WT, l2wt)):
                sp.dma_start(dst[:, :, :], src).then_inc(sem("setup_loaded"), 16)
            sp.dma_start(COLS[:, :], cols).then_inc(sem("setup_loaded"), 16)

            def load(s, k, n):
                i = STREAMS.index(s)
                if n is not None:
                    sp.wait_ge(sem("rest_ready", s), n)
                sp.dma_start(X[s][:, :, :], xs[k, i]).then_inc(sem("x_loaded", s), 16)
                if n is not None:
                    sp.wait_ge(sem("p6U", s), n)
                sp.dma_start(T[s][:, :, :], adj_t[k, i]).then_inc(sem("t_loaded", s), 16)
                sp.dma_start(R[s][:, :, :], adj_r[k, i]).then_inc(sem("r_loaded", s), 16)
                sp.dma_start(WR[s][:, :, :], adj_w[k, i].partition_broadcast(P)).then_inc(sem("w_loaded", s), 16)

            def store(s, k, n):
                sp.wait_ge(sem("c6W", s), n)
                sp.dma_start(out[k, STREAMS.index(s)], O[s][:, :, :]).then_inc(sem("stored", s), 16)

            load("A", 0, None)
            for dst, src in ((B1, b1), (B2, b2)):
                sp.dma_start(dst[:, :], src.partition_broadcast(P)).then_inc(sem("bias_loaded"), 16)
            load("B", 0, None)
            for dst, src in ((L1W, l1w), (L2W, l2w), (L3W1, l3w1), (L3W2, l3w2), (L3W3, l3w3)):
                sp.dma_start(dst[:, :, :], src).then_inc(sem("weights_loaded"), 16)
            for dst, src in ((L1B, l1b), (L3B1, l3b1), (L3B2, l3b2), (L3B3, l3b3)):
                sp.dma_start(dst[:, :], src.partition_broadcast(P)).then_inc(sem("weights_loaded"), 16)
            with sp.Fori(1, GROUPS) as k:
                for s in STREAMS:
                    n = sp.snap(2 * J * k + done_at(s, -1, J - 1))
                    load(s, k, n)
                    store(s, k - 1, n)
            for s in STREAMS:
                store(s, GROUPS - 1, done_at(s, GROUPS - 1, J - 1))
            for s in STREAMS:
                sp.wait_ge(sem("stored", s), 16 * (GROUPS + 1))

        @block.tensor
        def _(pe):
            pe.wait_ge(sem("spread_ready"), 1)
            for m in range(HC):
                last = nc.tensor.matmul(WB[0][:, 0:D], SPREAD[:, m, :], W2[:, m, :], start=(m == 0), stop=(m == HC - 1))
            last.then_inc(sem("bw_product"), 1)
            for m in range(DC):
                last = nc.tensor.matmul(UB[0][:, 0:D], SPREAD[:, HC + m, :], L2WT[:, m, :], start=(m == 0),
                                        stop=(m == DC - 1))
            last.then_inc(sem("wa_product"), 1)
            pe.wait_ge(sem("bwwa_ready"), 1)
            pe.wait_ge(sem("weights_loaded"), 9 * 16)
            pe.wait_ge(sem("w2g_ready"), 1)

            def bank_free(s, step, c, k, j, kind):
                steps = [x for x in PE_ORDER if x[1] in kind]
                taken = [x for x in steps if isinstance(k, dict) or bool(x[2]) == bool(k)]
                n = [x[:2] for x in taken].index((s, step))
                if n:
                    s0, step0, back0 = taken[n - 1]
                elif k == 0:
                    return
                else:
                    s0, step0, back0 = steps[-1]
                    back0 -= 1
                value = k[s0, back0]["v"][j] if isinstance(k, dict) else done_at(s0, k + back0, j)
                pe.wait_ge(sem(f"c{step0}"), value)

            U_STEPS = ("G", "3S") + tuple(f"{i}U" for i in range(7))
            W_STEPS = tuple(f"{i}W" for i in range(7))

            def unit(step, lhs, rhs, chunks):
                def f(s, c, k):
                    for j in range(J):
                        if step in U_WAITS:
                            pe.wait_ge(sem(U_WAITS[step], s), c["v"][j])
                        if step in U_WAITS2:
                            pe.wait_ge(sem(U_WAITS2[step], s), c["v"][j])
                        bank_free(s, step, c, k, j, U_STEPS)
                        for m in range(chunks):
                            last = nc.tensor.matmul(UB[j][:, m * P:(m + 1) * P], lhs(s, j)[:, m * P:(m + 1) * P],
                                                    rhs(s, j), start=True, stop=True)
                        last.then_inc(sem(f"p{step}", s), 1)
                return f

            def weigh(step, weights, chunks, n):
                def f(s, c, k):
                    for j in range(J):
                        pe.wait_ge(sem(f"c{step[0]}U", s), c["v"][j])
                        bank_free(s, step, c, k, j, W_STEPS)
                        for m in range(chunks):
                            last = nc.tensor.matmul(WB[j][:, 0:n], U[s][:, j, m * P:(m + 1) * P], weights[:, m, :],
                                                    start=(m == 0), stop=(m == chunks - 1))
                        last.then_inc(sem(f"p{step}", s), 1)
                return f

            U_WAITS = {"G": "bht_ready", "0U": "h0_ready", "1U": "z_ready", "2U": "h1_ready", "3S": "diag_ready",
                       "3U": "ae_ready", "4U": "h3_ready", "5U": "h4_ready", "6U": "h5_ready"}
            U_WAITS2 = {"0U": "cG", "2U": "at_ready"}
            parts = {
                "G": unit("G", lambda s, j: HT[s][:, j, :], lambda s, j: BHT[s][:, j, :], 1),
                "0U": unit("0U", lambda s, j: H[s][:, j, :], lambda s, j: G[s][:, j, :], DC),
                "1U": unit("1U", lambda s, j: Z[s][:, j, :], lambda s, j: G[s][:, j, :], HC),
                "2U": unit("2U", lambda s, j: H[s][:, j, :], lambda s, j: AT[s][:, j, :], DC),
                "3S": unit("3S", lambda s, j: ONES[:, :], lambda s, j: TMP[s][:, j, 0:P], 1),
                "3U": unit("3U", lambda s, j: H[s][:, j, :], lambda s, j: AE[s][:, j, :], DC),
                "4U": unit("4U", lambda s, j: H[s][:, j, :], lambda s, j: T[s][:, j, :], DC),
                "5U": unit("5U", lambda s, j: H[s][:, j, :], lambda s, j: T[s][:, j, :], DC),
                "6U": unit("6U", lambda s, j: H[s][:, j, :], lambda s, j: T[s][:, j, :], DC),
                "0W": weigh("0W", W1, DC, DH), "1W": weigh("1W", W2G, HC, D), "2W": weigh("2W", L1W, DC, D),
                "3W": weigh("3W", L2W, DC, D), "4W": weigh("4W", L3W1, DC, D), "5W": weigh("5W", L3W2, DC, D),
                "6W": weigh("6W", L3W3, DC, D)}

            run(pe, PE_ORDER, parts)

        @block.scalar
        def _(act):
            def take(step, dst, n):
                def f(s, c, k):
                    for j in range(J):
                        act.wait_ge(sem(f"p{step}", s), c["v"][j])
                        nc.scalar.activation(dst[s][:, j, 0:n], UB[j][:, 0:n], ACT.Copy).then_inc(sem(f"c{step}", s), 1)
                return f

            def normalise(s, c, src, waits, done):
                for j in range(J):
                    act.wait_ge(sem(waits, s), c["v"][j])
                    nc.scalar.activation(H[s][:, j, :], src[s][:, j, :], ACT.Relu, bias=NB[s][:, j:j + 1],
                                         scale=LN[s][:, RSTD, j:j + 1]).then_inc(sem(done, s), 1)

            def prep(s, c, k):
                normalise(s, c, X, "ln0_ready", "h0_ready")
                act.wait_ge(sem("r_loaded", s), c["dma"])
                for j in range(J):
                    nc.scalar.activation(JUNK[s][:, j, 2, :], R[s][:, j, :], ACT.Copy,
                                         accum_out=ST[s][:, RSR, j:j + 1]).then_inc(sem("rsr_ready", s), 1)

            def gcn(s, c, k):
                for j in range(J):
                    act.wait_ge(sem("c2W", s), c["v"][j])
                    nc.scalar.activation(TMP[s][:, j, :], TMP[s][:, j, :], ACT.Tanh).then_inc(sem("tanh_ready", s), 1)
                normalise(s, c, RES, "ln2_ready", "h2_ready")

            def scores(s, c, k):
                for j in range(J):
                    act.wait_ge(sem("p3S", s), c["v"][j])
                    act.wait_ge(sem("s8_ready", s), c["v"][j])
                    nc.scalar.activation(E[s][:, j, :], UB[j][:, 0:P], ACT.Tanh, bias=ST[s][:, S8, j:j + 1],
                                         scale=0.125).then_inc(sem("c3S", s), 1)
                for j in range(J):
                    act.wait_ge(sem("leak_ready", s), c["v"][j])
                    nc.scalar.activation(E[s][:, j, :], E[s][:, j, :], ACT.Exp, scale=8.0).then_inc(sem("e_ready", s), 1)

            def relu(step, waits, done):
                def f(s, c, k):
                    for j in range(J):
                        act.wait_ge(sem(waits, s), c["v"][j])
                        nc.scalar.activation(H[s][:, j, :], TMP[s][:, j, :], ACT.Relu).then_inc(sem(done, s), 1)
                return f

            parts = {"P": prep, "G": take("G", G, P), "0U": take("0U", U, D), "1U": take("1U", U, DH),
                     "2U": take("2U", U, D), "3U": take("3U", U, D), "4U": take("4U", U, D), "5U": take("5U", U, D),
                     "6U": take("6U", U, D), "1W": lambda s, c, k: normalise(s, c, RES, "ln1_ready", "h1_ready"),
                     "2W": gcn, "3S": scores, "3W": lambda s, c, k: normalise(s, c, RES, "ln3_ready", "h3_ready"),
                     "4W": relu("4W", "c4W", "h4_ready"), "5W": relu("5W", "c5W", "h5_ready")}
            run(act, ACT_ORDER, parts)

        @block.vector
        def _(dve):
            dve.wait_ge(sem("setup_loaded"), 64)
            dve.wait_ge(sem("ones_ready"), 1)
            for m in range(HC):
                nc.vector.tensor_scalar(SPREAD[:, m, :], ONES[:, :], BETA[:, m:m + 1], None, ALU.mult)
                nc.vector.tensor_scalar(W2G[:, m, :], W2[:, m, :], GAMMA[:, m:m + 1], None, ALU.mult)\
                    .then_inc(sem("w2g_parts"), 1)
            for m in range(DC):
                last = nc.vector.tensor_scalar(SPREAD[:, HC + m, :], ONES[:, :], ACOL[:, m:m + 1], None, ALU.mult)
            last.then_inc(sem("spread_ready"), 1)
            dve.wait_ge(sem("w2g_parts"), HC)
            dve.wait_ge(sem("bw_product"), 1)
            nc.vector.tensor_copy(BW[:, :], WB[0][:, 0:D]).then_inc(sem("w2g_ready"), 1)
            dve.wait_ge(sem("wa_product"), 1)
            nc.vector.tensor_copy(WA[:, :], UB[0][:, 0:D]).then_inc(sem("bwwa_ready"), 1)
            dve.wait_ge(sem("bwwa_ready"), 1)
            dve.wait_ge(sem("w2g_ready"), 1)
            dve.wait_ge(sem("ident_ready"), 1)
            dve.wait_ge(sem("bias_loaded"), 32)
            dve.wait_ge(sem("weights_loaded"), 9 * 16)

            def stats(s, c, src, n, tag):
                for j in range(J):
                    nc.vector.bn_stats(BN[s][:, j, :], src(j)).then_inc(sem("bn_stats" + tag), 1)
                mean0, sq0, mean1, sq1 = (BN[s][:, :, i] for i in (1, 2, 4, 5))
                f = lambda i: LN[s][:, i, :]
                dve.wait_ge(sem("bn_stats" + tag), c["v"][J - 1])
                nc.vector.tensor_tensor(f(SUM), mean0, mean1, ALU.add)
                nc.vector.scalar_tensor_tensor(f(M2), sq0, n * LN_EPS, sq1, ALU.add, ALU.add)
                nc.vector.tensor_tensor(f(DIF), mean0, mean1, ALU.subtract).then_inc(sem("mean_dif" + tag), 4)
                dve.wait_ge(sem("mean_dif" + tag), c["v"][J - 1])
                nc.vector.scalar_tensor_tensor(f(DSQ), f(DIF), 0.25, f(DIF), ALU.mult, ALU.mult)
                nc.vector.tensor_scalar(f(NMU), f(SUM), -0.5, None, ALU.mult).then_inc(sem("mean_dsq" + tag), 4)
                dve.wait_ge(sem("mean_dsq" + tag), c["v"][J - 1])
                nc.vector.scalar_tensor_tensor(f(VE), f(M2), 1.0 / n, f(DSQ), ALU.mult, ALU.add)\
                    .then_inc(sem("mv_ready" + tag), 4)

            def prep(s, c, k):
                v4 = c["v"][J - 1]
                dve.wait_ge(sem("x_loaded", s), c["dma"])
                stats(s, c, lambda j: X[s][:, j, :], D, "0")
                dve.wait_ge(sem("t_loaded", s), c["dma"])
                for j in range(J):
                    nc.vector.tensor_scalar(HT[s][:, j, :], T[s][:, j, :], 0.0, 0.0, ALU.not_equal, ALU.add,
                                            accum_out=ST[s][:, CNT, j:j + 1]).then_inc(sem("ht_ready", s), 1)
                dve.wait_ge(sem("ht_ready", s), v4)
                nc.vector.tensor_scalar(ST[s][:, CNM, :], ST[s][:, CNT, :], 1.0, None, ALU.max).then_inc(sem("cnm", s), 4)
                dve.wait_ge(sem("cnm", s), v4)
                nc.vector.reciprocal(ST[s][:, BE, :], ST[s][:, CNM, :]).then_inc(sem("be", s), 4)
                dve.wait_ge(sem("be", s), v4)
                for j in range(J):
                    nc.vector.tensor_scalar(BHT[s][:, j, :], HT[s][:, j, :], ST[s][:, BE, j:j + 1], None,
                                            ALU.mult).then_inc(sem("bht_ready", s), 1)
                dve.wait_ge(sem("r_loaded", s), c["dma"])
                dve.wait_ge(sem("w_loaded", s), c["dma"])
                for j in range(J):
                    nc.vector.tensor_scalar(JUNK[s][:, j, 0, :], R[s][:, j, :], 0.0, 0.0, ALU.not_equal, ALU.add,
                                            accum_out=ST[s][:, DGH, j:j + 1]).then_inc(sem("hr_ready", s), 1)
                for j in range(J):
                    nc.vector.scalar_tensor_tensor(JUNK[s][:, j, 1, :], R[s][:, j, :], 0.0, WR[s][:, j, :],
                                                   ALU.not_equal, ALU.mult, accum_out=ST[s][:, DNS, j:j + 1])\
                        .then_inc(sem("dns", s), 1)
                for j in range(J):
                    dve.wait_ge(sem("hr_ready", s), c["v"][j])
                    nc.vector.scalar_tensor_tensor(JUNK[s][:, j, 0, :], JUNK[s][:, j, 0, :], 1.0, IDENT[:, :],
                                                   ALU.mult, ALU.mult, accum_out=ST[s][:, DGI, j:j + 1])\
                        .then_inc(sem("dgi", s), 1)
                dve.wait_ge(sem("dns", s), v4)
                nc.vector.tensor_scalar(ST[s][:, DN, :], ST[s][:, DNS, :], TINY, None, ALU.max).then_inc(sem("dnm", s), 4)
                dve.wait_ge(sem("dgi", s), v4)
                nc.vector.scalar_tensor_tensor(ST[s][:, DG1, :], ST[s][:, DGH, :], 1.0, ST[s][:, DGI, :], ALU.add,
                                               ALU.subtract).then_inc(sem("deg_ready", s), 4)
                dve.wait_ge(sem("dnm", s), v4)
                nc.vector.reciprocal(ST[s][:, DNI, :], ST[s][:, DN, :]).then_inc(sem("dni", s), 4)
                dve.wait_ge(sem("dni", s), v4)
                nc.vector.scalar_tensor_tensor(ST[s][:, DN, :], ST[s][:, DNS, :], 0.0, ST[s][:, DNI, :], ALU.is_gt,
                                               ALU.mult).then_inc(sem("dn_ready", s), 4)
                dve.wait_ge(sem("dn_ready", s), v4)
                nc.vector.tensor_tensor(ST[s][:, S2, :], ST[s][:, DN, :], ST[s][:, DGH, :], ALU.mult)\
                    .then_inc(sem("s2", s), 4)
                dve.wait_ge(sem("s2", s), v4)
                for j in range(J):
                    nc.vector.scalar_tensor_tensor(RES[s][:, j, :], BW[:, :], ST[s][:, S2, j:j + 1], X[s][:, j, :],
                                                   ALU.mult, ALU.add).then_inc(sem("rest_begun", s), 1)

            def hidden(s, c, k):
                for j in range(J):
                    dve.wait_ge(sem("p0W", s), c["v"][j])
                    nc.vector.scalar_tensor_tensor(Z[s][:, j, :], WB[j][:, 0:DH], ST[s][:, DN, j:j + 1], B1[:, :],
                                                   ALU.mult, ALU.add).then_inc(sem("c0W", s), 1)
                for j in range(J):
                    dve.wait_ge(sem("c0W", s), c["v"][j])
                    nc.vector.tensor_scalar(Z[s][:, j, :], Z[s][:, j, :], 0.0, None, ALU.max)\
                        .then_inc(sem("hidden_relu", s), 1)

            def hidden_norm(s, c, k):
                dve.wait_ge(sem("hidden_relu", s), c["v"][J - 1])
                stats(s, c, lambda j: Z[s][:, j, :], DH, "z")
                for j in range(J):
                    dve.wait_ge(sem("lnz_ready", s), c["v"][j])
                    nc.vector.tensor_scalar(Z[s][:, j, :], Z[s][:, j, :], LN[s][:, RSTD, j:j + 1], NB[s][:, j:j + 1], ALU.mult,
                                            ALU.add).then_inc(sem("z_ready", s), 1)

            def conv_out(s, c, k):
                for j in range(J):
                    dve.wait_ge(sem("p1W", s), c["v"][j])
                    dve.wait_ge(sem("rest_ready", s), c["v"][j])
                    nc.vector.scalar_tensor_tensor(RES[s][:, j, :], WB[j][:, 0:D], ST[s][:, DN, j:j + 1],
                                                   RES[s][:, j, :], ALU.mult, ALU.add).then_inc(sem("c1W", s), 1)
                dve.wait_ge(sem("c1W", s), c["v"][J - 1])
                stats(s, c, lambda j: RES[s][:, j, :], D, "1")

            def gcn_out(s, c, k):
                for j in range(J):
                    dve.wait_ge(sem("p2W", s), c["v"][j])
                    nc.vector.scalar_tensor_tensor(TMP[s][:, j, :], WB[j][:, 0:D], ST[s][:, DINV, j:j + 1], L1B[:, :],
                                                   ALU.mult, ALU.add).then_inc(sem("c2W", s), 1)
                for j in range(J):
                    dve.wait_ge(sem("tanh_ready", s), c["v"][j])
                    nc.vector.tensor_tensor(RES[s][:, j, :], RES[s][:, j, :], TMP[s][:, j, :], ALU.add)\
                        .then_inc(sem("x2_ready", s), 1)
                dve.wait_ge(sem("x2_ready", s), c["v"][J - 1])
                stats(s, c, lambda j: RES[s][:, j, :], D, "2")
                for j in range(J):
                    dve.wait_ge(sem("h2_ready", s), c["v"][j])
                    nc.vector.scalar_tensor_tensor(Z[s][:, j, 0:D], H[s][:, j, :], 1.0, WA[:, :], ALU.mult, ALU.mult,
                                                   accum_out=ST[s][:, SC, j:j + 1]).then_inc(sem("s_ready", s), 1)
                for j in range(J):
                    dve.wait_ge(sem("s_ready", s), c["v"][j])
                    nc.vector.tensor_scalar(TMP[s][:, j, 0:P], IDENT[:, :], ST[s][:, SC, j:j + 1], None, ALU.mult)\
                        .then_inc(sem("diag_ready", s), 1)

            def scores(s, c, k):
                for j in range(J):
                    dve.wait_ge(sem("c3S", s), c["v"][j])
                    nc.vector.scalar_tensor_tensor(E[s][:, j, :], E[s][:, j, :], 0.1, E[s][:, j, :], ALU.mult,
                                                   ALU.max).then_inc(sem("leak_ready", s), 1)
                for j in range(J):
                    dve.wait_ge(sem("e_ready", s), c["v"][j])
                    nc.vector.tensor_tensor(AE[s][:, j, :], E[s][:, j, :], T[s][:, j, :], ALU.mult)\
                        .then_inc(sem("ae_ready", s), 1)
                for j in range(J):
                    nc.vector.scalar_tensor_tensor(JUNK[s][:, j, 1, :], E[s][:, j, :], 1.0, R[s][:, j, :], ALU.mult,
                                                   ALU.mult, accum_out=ST[s][:, RSA, j:j + 1])\
                        .then_inc(sem("rsa", s), 1)
                dve.wait_ge(sem("rsa", s), c["v"][J - 1])
                nc.vector.reciprocal(ST[s][:, RSA, :], ST[s][:, RSA, :]).then_inc(sem("rsa_inv", s), 4)
                dve.wait_ge(sem("rsa_inv", s), c["v"][J - 1])
                dve.wait_ge(sem("rsr_ready", s), c["v"][J - 1])
                nc.vector.tensor_tensor(ST[s][:, RR, :], ST[s][:, RSA, :], ST[s][:, RSR, :], ALU.mult)\
                    .then_inc(sem("rr_ready", s), 4)

            def attention_out(s, c, k):
                dve.wait_ge(sem("rr_ready", s), c["v"][J - 1])
                for j in range(J):
                    dve.wait_ge(sem("p3W", s), c["v"][j])
                    nc.vector.scalar_tensor_tensor(RES[s][:, j, :], WB[j][:, 0:D], ST[s][:, RR, j:j + 1],
                                                   RES[s][:, j, :], ALU.mult, ALU.add).then_inc(sem("c3W", s), 1)
                dve.wait_ge(sem("c3W", s), c["v"][J - 1])
                stats(s, c, lambda j: RES[s][:, j, :], D, "3")

            def add_bias(step, bias):
                def f(s, c, k):
                    for j in range(J):
                        dve.wait_ge(sem(f"p{step}", s), c["v"][j])
                        nc.vector.tensor_tensor(TMP[s][:, j, :], WB[j][:, 0:D], bias[:, :], ALU.add)\
                            .then_inc(sem(f"c{step}", s), 1)
                return f

            def last_out(s, c, k):
                dve.wait_ge(sem("stored", s), c["dma"])
                for j in range(J):
                    dve.wait_ge(sem("p6W", s), c["v"][j])
                    dve.wait_ge(sem("x3b_ready", s), c["v"][j])
                    nc.vector.tensor_tensor(O[s][:, j, :], WB[j][:, 0:D], RES[s][:, j, :], ALU.add)\
                        .then_inc(sem("c6W", s), 1)

            parts = {"P": prep, "0W": hidden, "0N": hidden_norm, "1W": conv_out, "2W": gcn_out, "3S": scores,
                     "3W": attention_out, "4W": add_bias("4W", L3B1), "5W": add_bias("5W", L3B2), "6W": last_out}
            run(dve, DVE_ORDER, parts)

        @block.gpsimd
        def _(pool):
            nc.gpsimd.memset(ONES[:, :], 1.0).then_inc(sem("ones_ready"), 1)
            nc.gpsimd.memset(EIGHTH[:, :], 0.125)
            for s in STREAMS:
                nc.gpsimd.memset(NB[s][:, :], 0.0).then_inc(sem("stored", s), 16)
            nc.gpsimd.memset(MHALF[:, :], -0.5).then_inc(sem("mhalf_ready"), 1)
            nc.gpsimd.memset(IDENT[:, :], 0.0).then_inc(sem("zeros_ready"), 1)
            pool.wait_ge(sem("zeros_ready"), 1)
            nc.gpsimd.affine_select(out=IDENT[:, :], in_=IDENT[:, :], compare_op=ALU.not_equal, fill=1.0, base=0,
                                    pattern=[[-1, P]], channel_multiplier=1).then_inc(sem("ident_ready"), 1)
            pool.wait_ge(sem("ident_ready"), 1)
            nc.gpsimd.tensor_tensor(OFFDIAG[:, :], ONES[:, :], IDENT[:, :], ALU.subtract).then_inc(sem("offdiag_ready"), 1)
            pool.wait_ge(sem("mhalf_ready"), 1)
            pool.wait_ge(sem("offdiag_ready"), 1)
            pool.wait_ge(sem("bias_loaded"), 32)
            pool.wait_ge(sem("weights_loaded"), 9 * 16)

            def norm(s, c, tag, scale=None):
                v4, rstd = c["v"][J - 1], LN[s][:, RSTD, :]
                pool.wait_ge(sem("mv_ready" + tag), v4)
                nc.gpsimd.tensor_tensor(rstd, LN[s][:, VE, :], MHALF[:, :], ALU.pow).then_inc(sem("rstd" + tag), 4)
                pool.wait_ge(sem("rstd" + tag), v4)
                if scale is not None:
                    nc.gpsimd.tensor_tensor(rstd, rstd, scale, ALU.mult).then_inc(sem("rstd_scaled"), 4)
                    pool.wait_ge(sem("rstd_scaled"), v4)
                nc.gpsimd.tensor_tensor(NB[s][:, :], LN[s][:, NMU, :], rstd, ALU.mult).then_inc(sem(f"ln{tag}_ready"), 4)

            def prep(s, c, k):
                norm(s, c, "0")
                for j in range(J):
                    pool.wait_ge(sem("ht_ready", s), c["v"][j])
                    nc.gpsimd.tensor_tensor(AT[s][:, j, :], HT[s][:, j, :], OFFDIAG[:, :], ALU.mult)\
                        .then_inc(sem("at_offdiag", s), 1)
                for j in range(J):
                    pool.wait_ge(sem("at_offdiag", s), c["v"][j])
                    nc.gpsimd.tensor_tensor(AT[s][:, j, :], AT[s][:, j, :], IDENT[:, :], ALU.add)\
                        .then_inc(sem("at_ready", s), 1)
                pool.wait_ge(sem("deg_ready", s), c["v"][J - 1])
                nc.gpsimd.tensor_tensor(ST[s][:, DINV, :], ST[s][:, DG1, :], MHALF[:, :], ALU.pow)\
                    .then_inc(sem("dinv", s), 4)

            def rest(s, c, k):
                for j in range(J):
                    pool.wait_ge(sem("rest_begun", s), c["v"][j])
                    nc.gpsimd.tensor_tensor(RES[s][:, j, :], RES[s][:, j, :], B2[:, :], ALU.add)\
                        .then_inc(sem("rest_b2", s), 1)
                for j in range(J):
                    pool.wait_ge(sem("rest_b2", s), c["v"][j])
                    pool.wait_ge(sem("h0_ready", s), c["v"][j])
                    nc.gpsimd.tensor_tensor(RES[s][:, j, :], RES[s][:, j, :], H[s][:, j, :], ALU.add)\
                        .then_inc(sem("rest_ready", s), 1)

            def conv(s, c, k):
                pool.wait_ge(sem("dinv", s), c["v"][J - 1])
                norm(s, c, "1", ST[s][:, DINV, :])

            def gcn(s, c, k):
                norm(s, c, "2")
                pool.wait_ge(sem("s_ready", s), c["v"][J - 1])
                nc.gpsimd.tensor_tensor(ST[s][:, S8, :], ST[s][:, SC, :], EIGHTH[:, :], ALU.mult)\
                    .then_inc(sem("s8_ready", s), 4)

            def attention(s, c, k):
                norm(s, c, "3")
                for j in range(J):
                    pool.wait_ge(sem("h3_ready", s), c["v"][j])
                    nc.gpsimd.tensor_tensor(RES[s][:, j, :], RES[s][:, j, :], L3B3[:, :], ALU.add)\
                        .then_inc(sem("x3b_ready", s), 1)

            parts = {"P": prep, "R": rest, "0N": lambda s, c, k: norm(s, c, "z"), "1W": conv, "2W": gcn,
                     "3W": attention}
            run(pool, POOL_ORDER, parts)


def kernel(x, adj, L0_gnn_W1, L0_gnn_b1, L0_gnn_gamma, L0_gnn_beta, L0_gnn_W2, L0_gnn_b2, L1_gnn_W, L1_gnn_b,
           L2_gnn_w, L2_gnn_a, L3_gnn_W1, L3_gnn_b1, L3_gnn_W2, L3_gnn_b2, L3_gnn_W3, L3_gnn_b3):
    import numpy as np
    import concourse.bacc as bacc
    from concourse.bass_utils import run_bass_kernel_spmd as launch

    x, adj = np.asarray(x), np.asarray(adj)
    n, c, d = x.shape
    g = n // (2 * J)

    def grouped(a):
        return a.reshape(g, 2, J, a.shape[1], a.shape[2]).transpose(0, 1, 3, 2, 4)

    def chunked(w):
        w = np.asarray(w)
        return w.reshape(-1, P, w.shape[1]).transpose(1, 0, 2)

    def column(v):
        return np.asarray(v).reshape(-1, P).T

    arrays = {
        "xs": grouped(x), "adj_t": grouped(adj.transpose(0, 2, 1)), "adj_r": grouped(adj),
        "adj_w": adj[:, 0, :].reshape(g, 2, J, c),
        "w1t": chunked(np.asarray(L0_gnn_W1).T), "w2t": chunked(np.asarray(L0_gnn_W2).T), "l1w": chunked(L1_gnn_W),
        "l2w": chunked(L2_gnn_w), "l2wt": chunked(np.asarray(L2_gnn_w).T), "l3w1": chunked(L3_gnn_W1),
        "l3w2": chunked(L3_gnn_W2), "l3w3": chunked(L3_gnn_W3),
        "cols": np.concatenate([column(L0_gnn_gamma), column(L0_gnn_beta), column(L2_gnn_a)], axis=1),
        "b1": L0_gnn_b1, "b2": L0_gnn_b2, "l1b": L1_gnn_b, "l3b1": L3_gnn_b1, "l3b2": L3_gnn_b2, "l3b3": L3_gnn_b3}
    arrays = {k: np.ascontiguousarray(np.asarray(a)) for k, a in arrays.items()}
    nc = bacc.Bacc("TRN2", target_bir_lowering=False, num_devices=1)
    args = {k: nc.dram_tensor(f"in_{k}", a.shape, mybir.dt.from_np(a.dtype), kind="ExternalInput").ap()
            for k, a in arrays.items()}
    out = nc.dram_tensor("out_rows", arrays["xs"].shape, F32, kind="ExternalOutput").ap()
    program(nc, **args, out=out)
    r = launch(nc, [{f"in_{k}": a for k, a in arrays.items()}], core_ids=[0])
    rows = r.results[0]["out_rows"]
    return rows.transpose(0, 1, 3, 2, 4).reshape(n, c, d)
```

```python
from contextlib import ExitStack

import concourse.bass as bass
from concourse import mybir
from concourse.alu_op_type import AluOpType as ALU

F32 = mybir.dt.float32
F32R = mybir.dt.float32r
ACT = mybir.ActivationFunctionType
P = 128
J = 2
STREAMS = ("A", "B", "C", "D")
LN_EPS = 1e-5
HALF = 32
TINY = 1.1754944e-38

PE_SLOTS = {
    "G": 0.883, "0U": 1.331, "0W": 2.220, "1U": 3.316, "1W": 3.666, "2U": 5.716, "2W": 6.069, "3S": 8.190,
    "3U": 8.247, "3W": 8.923, "4U": 10.150, "4W": 10.474, "5U": 11.193, "5W": 11.830, "6U": 11.936, "6W": 12.423}
ACT_SLOTS = {
    "P": 0.92, "P2": 0.80, "P3": 3.14, "B": 0.89, "XB": 1.86, "G": 0.99, "0U": 1.48, "0W": 2.82, "0Z": 3.36,
    "1U": 3.64, "1W": 5.55, "2U": 5.75, "2W": 6.59, "2X": 7.26, "3S": 7.77, "3E": 7.88, "3U": 8.66, "3W": 9.88,
    "4U": 10.19, "4W": 10.72, "5U": 11.09, "5W": 11.98, "6U": 12.18}
DVE_SLOTS = {
    "P": 0.354, "PT": 0.588, "P2": 1.527, "0U": 1.465, "0W": 2.092, "0N": 2.784, "1U": 3.583, "1W": 3.810,
    "1N": 4.532, "2U": 5.520, "2W": 6.155, "2X": 6.722, "2S": 7.165, "2D": 7.204, "3S": 7.643, "3E": 7.921,
    "3R": 7.805, "3I": 8.166, "3U": 8.362, "3W": 9.010, "3N": 9.042, "4U": 10.003, "5U": 11.068, "6U": 12.111,
    "6W": 12.794}
POOL_SLOTS = {
    "P": 0.59, "AT": 1.14, "DI": 2.00, "R": 2.29, "0N": 2.64, "1W": 4.55, "2A": 6.25, "2X": 6.85, "2S": 7.21,
    "3W": 9.10, "X3": 9.81}
SLOTS = 12


def ordered(slots):
    entries = []
    for i, s in enumerate(STREAMS):
        for step, at in slots.items():
            at += i * SLOTS / len(STREAMS)
            entries.append((at % SLOTS, s, step, -int(at // SLOTS)))
    return [x[1:] for x in sorted(entries)]


PE_ORDER, ACT_ORDER, DVE_ORDER, POOL_ORDER = map(ordered, (PE_SLOTS, ACT_SLOTS, DVE_SLOTS, POOL_SLOTS))


def program(nc, xs, adj_t, adj_r, adj_w, w1t, w2t, l1w, l2w, l2wt, l3w1, l3w2, l3w3,
            cols, b1, b2, l1b, l3b1, l3b2, l3b3, out):
    GROUPS = xs.shape[0]
    D = l1w.shape[2]
    DC = D // P
    DH = w1t.shape[2]
    HC = DH // P

    with ExitStack() as ctx:
        def sb(name, shape, dt=F32):
            return ctx.enter_context(nc.sbuf_tensor(name, shape, dt))

        sems = {}
        PER_STREAM = ("x_loaded", "t_loaded", "r_loaded", "w_loaded", "stored")

        def sem(name, s=""):
            key = f"{name}_{s}" if name in PER_STREAM else name
            if key not in sems:
                sems[key] = ctx.enter_context(nc.semaphore(key))
            return sems[key]

        WIDTH = {"0W": (DC, DH), "1W": (HC, D), "2W": (DC, D), "3W": (DC, D), "4W": (DC, D), "5W": (DC, D), "6W": (DC, D)}
        WHI = {step: sb(f"WHI{step}", [P, *shape], F32R) for step, shape in WIDTH.items()}
        WLO = {step: sb(f"WLO{step}", [P, *shape], F32R) for step, shape in WIDTH.items()}
        COLS = sb("COLS", [P, 2 * HC + DC])
        GAMMA, BETA, ACOL = COLS[:, 0:HC], COLS[:, HC:2 * HC], COLS[:, 2 * HC:]
        B1 = sb("B1", [P, DH])
        B2, L1B, L3B1, L3B2, L3B3 = (sb(n, [P, D]) for n in ("B2", "L1B", "L3B1", "L3B2", "L3B3"))
        BIAS = {step: sb(f"BIAS{step}", [2 * HALF, D], F32R) for step in ("4W", "5W")}
        SHARES = sb("SHARES", [2 * HALF, P], F32R)
        BW = sb("BW", [P, D])
        WA = sb("WA", [P, D])
        SPREAD = sb("SPREAD", [P, HC + DC, P])
        IDENT = sb("IDENT", [P, P])
        ONES = sb("ONES", [P, P])
        OFFDIAG = sb("OFFDIAG", [P, P])
        MHALF = sb("MHALF", [P, J])
        EIGHTH = sb("EIGHTH", [P, J])
        EPS = sb("EPS", [P, J])

        def per_stream(name, *shape):
            return {s: sb(f"{name}_{s}", [P, *shape]) for s in STREAMS}

        X = per_stream("X", J, D)
        T = per_stream("T", J, P)
        R = per_stream("R", J, P)
        WR = per_stream("WR", J, P)
        HT = per_stream("HT", J, P)
        BHT = per_stream("BHT", J, P)
        AT = per_stream("AT", J, P)
        G = per_stream("G", J, P)
        JUNK = per_stream("JUNK", J, 5, P)
        H = per_stream("H", J, D)
        UHI = {s: sb(f"UHI_{s}", [P, J, DH], F32R) for s in STREAMS}
        ULO = {s: sb(f"ULO_{s}", [P, J, DH], F32R) for s in STREAMS}
        Z = per_stream("Z", J, DH)
        RES = per_stream("RES", J, D)
        TMP = per_stream("TMP", J, D)
        E = per_stream("E", J, P)
        AE = per_stream("AE", J, P)
        O = per_stream("O", J, D)
        BN = per_stream("BN", J, 6)
        MV = per_stream("MV", J, 2)
        LN = per_stream("LN", 4, J)
        SUM, VE, NMU, RSTD = range(4)
        NB = per_stream("NB", J)
        ST = per_stream("ST", 15, J)
        CNT, BE, DNS, DN, DNI, DGH, DG1, DINV, S2, RSR, RSA, RR, SC, S8, CNM = range(15)

        TURNS = 2
        UB = [[ctx.enter_context(nc.psum_tensor(f"UB{n}{j}", [P, 512], F32)) for j in range(J)] for n in range(TURNS)]
        WB = [[ctx.enter_context(nc.psum_tensor(f"WB{n}{j}", [P, 512], F32)) for j in range(J)] for n in range(TURNS)]
        U_STEPS = ("G", "3S") + tuple(f"{i}U" for i in range(7))
        W_STEPS = tuple(f"{i}W" for i in range(7))

        def bank(s, step, j):
            kind, banks = (U_STEPS, UB) if step in U_STEPS else (W_STEPS, WB)
            return banks[[x[:2] for x in PE_ORDER if x[1] in kind].index((s, step)) % TURNS][j]

        W2, W1 = (Z[s][:, :, :].rearrange("p j n -> p (j n)") for s in ("A", "B"))
        W1 = W1.rearrange("p (m n) -> p m n", n=DH)
        W2 = W2.rearrange("p (m n) -> p m n", n=D)
        L2WT, L1W, L2W, L3W1, L3W2, L3W3 = (x[:, :, :] for x in (TMP["A"], TMP["B"], TMP["C"], TMP["D"], O["C"], O["D"]))
        W2G = Z["C"][:, :, :].rearrange("p j n -> p (j n)").rearrange("p (m n) -> p m n", n=D)
        RAW = {"0W": W1, "1W": W2G, "2W": L1W, "3W": L2W, "4W": L3W1, "5W": L3W2, "6W": L3W3}

        block = ctx.enter_context(nc.Block())

        def done_at(s, k, j):
            return len(STREAMS) * J * k + J * STREAMS.index(s) + j + 1

        LIVE = [(s, back) for s in STREAMS for back in (0, -1)]

        def run(eng, order, parts):
            def values(k):
                return {(s, back): dict(v=[done_at(s, k + back, j) for j in range(J)], dma=16 * (k + back + 1))
                        for s, back in LIVE}

            for s, step, back in order:
                if not back:
                    parts[step](s, values(0)[s, 0], 0)
            with eng.Fori(1, GROUPS) as k:
                loop = {(s, back): dict(v=[eng.snap(len(STREAMS) * J * k + done_at(s, back, j)) for j in range(J)])
                        for s, back in LIVE}
                dma = {back: eng.snap(16 * k + 16 * (back + 1)) for back in (0, -1)}
                for s, back in LIVE:
                    loop[s, back]["dma"] = dma[back]
                for s, step, back in order:
                    parts[step](s, loop[s, back], loop)
            for s, step, back in order:
                if back:
                    parts[step](s, values(GROUPS)[s, back], GROUPS)

        @block.sync
        def _(sp):
            for dst, src in ((W2, w2t), (L2WT, l2wt), (W1, w1t), (L1W, l1w), (L2W, l2w), (L3W1, l3w1), (L3W2, l3w2),
                             (L3W3, l3w3)):
                sp.dma_start(dst, src).then_inc(sem("setup_loaded"), 16)
            sp.dma_start(COLS[:, :], cols).then_inc(sem("setup_loaded"), 16)

            def load(s, k, n):
                i = STREAMS.index(s)
                if n is not None:
                    sp.wait_ge(sem("rest_ready", s), n)
                sp.dma_start(X[s][:, :, :], xs[k, i]).then_inc(sem("x_loaded", s), 16)
                if n is not None:
                    sp.wait_ge(sem("p6U", s), n)
                sp.dma_start(T[s][:, :, :], adj_t[k, i]).then_inc(sem("t_loaded", s), 16)
                sp.dma_start(R[s][:, :, :], adj_r[k, i]).then_inc(sem("r_loaded", s), 16)
                sp.dma_start(WR[s][:, :, :], adj_w[k, i].partition_broadcast(P)).then_inc(sem("w_loaded", s), 16)

            def store(s, k, n):
                sp.wait_ge(sem("c6W", s), n)
                sp.dma_start(out[k, STREAMS.index(s)], O[s][:, :, :]).then_inc(sem("stored", s), 16)

            load("A", 0, None)
            for dst, src in ((B1, b1), (B2, b2), (L1B, l1b), (L3B1, l3b1), (L3B2, l3b2), (L3B3, l3b3)):
                sp.dma_start(dst[:, :], src.partition_broadcast(P)).then_inc(sem("bias_loaded"), 16)
            for s in STREAMS[1:]:
                load(s, 0, None)
            with sp.Fori(1, GROUPS) as k:
                for s in STREAMS:
                    n = sp.snap(len(STREAMS) * J * k + done_at(s, -1, J - 1))
                    load(s, k, n)
                    store(s, k - 1, n)
            for s in STREAMS:
                store(s, GROUPS - 1, done_at(s, GROUPS - 1, J - 1))
            for s in STREAMS:
                sp.wait_ge(sem("stored", s), 16 * (GROUPS + 1))

        @block.tensor
        def _(pe):
            pe.wait_ge(sem("spread_ready"), 1)
            for m in range(HC):
                last = nc.tensor.matmul(WB[0][0][:, 0:D], SPREAD[:, m, :], W2[:, m, :], start=(m == 0), stop=(m == HC - 1))
            last.then_inc(sem("bw_product"), 1)
            for m in range(DC):
                last = nc.tensor.matmul(UB[0][0][:, 0:D], SPREAD[:, HC + m, :], L2WT[:, m, :], start=(m == 0),
                                        stop=(m == DC - 1))
            last.then_inc(sem("wa_product"), 1)
            pe.wait_ge(sem("bwwa_ready"), 1)
            pe.wait_ge(sem("weights_split"), 1)

            def bank_free(s, step, c, k, j, kind):
                steps = [x for x in PE_ORDER if x[1] in kind]
                n = [x[:2] for x in steps].index((s, step))
                same = [(steps[m], 0) for m in range(n - TURNS, -1, -TURNS)]
                same += [(steps[m], 1) for m in range(len(steps) - 1, -1, -1) if (n - m) % TURNS == 0]
                for (s0, step0, back0), before in same:
                    if isinstance(k, dict):
                        value = k[s0, back0 - before]["v"][j]
                    else:
                        group = k - before + back0
                        if not 0 <= group < GROUPS:
                            continue
                        value = done_at(s0, group, j)
                    pe.wait_ge(sem(f"l{step0}" if step0[1:] == "U" else f"c{step0}"), value)
                    return

            def unit(step, lhs, rhs, chunks):
                def f(s, c, k):
                    for j in range(J):
                        if step in U_WAITS:
                            pe.wait_ge(sem(U_WAITS[step], s), c["v"][j])
                        if step in U_WAITS2:
                            pe.wait_ge(sem(U_WAITS2[step], s), c["v"][j])
                        bank_free(s, step, c, k, j, U_STEPS)
                        for m in range(chunks):
                            last = nc.tensor.matmul(bank(s, step, j)[:, m * P:(m + 1) * P], lhs(s, j)[:, m * P:(m + 1) * P],
                                                    rhs(s, j), start=True, stop=True)
                        last.then_inc(sem(f"p{step}", s), 1)
                return f

            def weigh(step):
                chunks, n = WIDTH[step]
                hi, lo = WHI[step], WLO[step]

                """(adjacency @ h) @ W, node-major."""
                def f(s, c, k):
                    for j in range(J):
                        pe.wait_ge(sem(f"l{step[0]}U"), c["v"][j])
                        bank_free(s, step, c, k, j, W_STEPS)
                        terms = [(u[s][:, j, m * P:(m + 1) * P], w[:, m, :]) for m in range(chunks)
                                 for u, w in ((ULO, hi), (UHI, lo), (UHI, hi))]
                        if step in BIAS:
                            terms.insert(0, (SHARES[:, :], BIAS[step][:, :]))
                        for i, (u, w) in enumerate(terms):
                            last = nc.tensor.matmul(bank(s, step, j)[:, 0:n], u, w, start=(i == 0),
                                                    stop=(i == len(terms) - 1))
                        last.then_inc(sem(f"p{step}", s), 1)
                return f

            U_WAITS = {"G": "bht_ready", "0U": "h0_ready", "1U": "z_ready", "2U": "h1_ready", "3S": "diag_ready",
                       "3U": "ae_ready", "4U": "h3_ready", "5U": "c4W", "6U": "c5W"}
            U_WAITS2 = {"0U": "cG", "2U": "at_ready"}
            parts = {
                "G": unit("G", lambda s, j: HT[s][:, j, :], lambda s, j: BHT[s][:, j, :], 1),
                "0U": unit("0U", lambda s, j: H[s][:, j, :], lambda s, j: G[s][:, j, :], DC),
                "1U": unit("1U", lambda s, j: Z[s][:, j, :], lambda s, j: G[s][:, j, :], HC),
                "2U": unit("2U", lambda s, j: H[s][:, j, :], lambda s, j: AT[s][:, j, :], DC),
                "3S": unit("3S", lambda s, j: ONES[:, :], lambda s, j: TMP[s][:, j, 0:P], 1),
                "3U": unit("3U", lambda s, j: H[s][:, j, :], lambda s, j: AE[s][:, j, :], DC),
                "4U": unit("4U", lambda s, j: H[s][:, j, :], lambda s, j: T[s][:, j, :], DC),
                "5U": unit("5U", lambda s, j: H[s][:, j, :], lambda s, j: T[s][:, j, :], DC),
                "6U": unit("6U", lambda s, j: H[s][:, j, :], lambda s, j: T[s][:, j, :], DC),
                **{step: weigh(step) for step in W_STEPS}}

            run(pe, PE_ORDER, parts)

        @block.scalar
        def _(act):
            def take(step, dst, n):
                def f(s, c, k):
                    for j in range(J):
                        act.wait_ge(sem(f"p{step}", s), c["v"][j])
                        nc.scalar.activation(dst[s][:, j, 0:n], bank(s, step, j)[:, 0:n], ACT.Copy).then_inc(sem(f"c{step}", s), 1)
                return f

            def normalise(s, c, src, waits, done):
                for j in range(J):
                    act.wait_ge(sem(waits, s), c["v"][j])
                    nc.scalar.activation(H[s][:, j, :], src[s][:, j, :], ACT.Relu, bias=NB[s][:, j:j + 1],
                                         scale=LN[s][:, RSTD, j:j + 1]).then_inc(sem(done, s), 1)

            def prep(s, c, k):
                normalise(s, c, X, "ln0_ready", "h0_ready")

            def by_members(s, c, k):
                for j in range(J):
                    act.wait_ge(sem("be"), c["v"][j])
                    nc.scalar.activation(BHT[s][:, j, :], HT[s][:, j, :], ACT.Copy, scale=ST[s][:, BE, j:j + 1])\
                        .then_inc(sem("bht_ready"), 1)

            def shift(s, c, k):
                for j in range(J):
                    act.wait_ge(sem("s2"), c["v"][j])
                    nc.scalar.activation(TMP[s][:, j, :], BW[:, :], ACT.Copy, scale=ST[s][:, S2, j:j + 1])\
                        .then_inc(sem("shift_ready"), 1)

            def node_degrees(s, c, k):
                act.wait_ge(sem("r_loaded", s), c["dma"])
                for j in range(J):
                    nc.scalar.activation(JUNK[s][:, j, 3, :], R[s][:, j, :], ACT.Sign).then_inc(sem("sign_ready"), 1)
                for j in range(J):
                    act.wait_ge(sem("sign_ready"), c["v"][j])
                    nc.scalar.activation(JUNK[s][:, j, 4, :], JUNK[s][:, j, 3, :], ACT.Square,
                                         accum_out=ST[s][:, DGH, j:j + 1]).then_inc(sem("dgh_ready"), 1)

            def row_sums(s, c, k):
                act.wait_ge(sem("r_loaded", s), c["dma"])
                for j in range(J):
                    nc.scalar.activation(JUNK[s][:, j, 2, :], R[s][:, j, :], ACT.Copy,
                                         accum_out=ST[s][:, RSR, j:j + 1]).then_inc(sem("rsr_ready", s), 1)

            def gcn(s, c, k):
                for j in range(J):
                    act.wait_ge(sem("c2W", s), c["v"][j])
                    nc.scalar.activation(TMP[s][:, j, :], TMP[s][:, j, :], ACT.Tanh).then_inc(sem("tanh_ready", s), 1)

            def scores(s, c, k):
                for j in range(J):
                    act.wait_ge(sem("p3S", s), c["v"][j])
                    act.wait_ge(sem("s8_ready", s), c["v"][j])
                    nc.scalar.activation(E[s][:, j, :], bank(s, "3S", j)[:, 0:P], ACT.Tanh, bias=ST[s][:, S8, j:j + 1],
                                         scale=0.125).then_inc(sem("c3S", s), 1)

            def exps(s, c, k):
                for j in range(J):
                    act.wait_ge(sem("leak_ready", s), c["v"][j])
                    nc.scalar.activation(E[s][:, j, :], E[s][:, j, :], ACT.Exp, scale=8.0).then_inc(sem("e_ready", s), 1)

            def hidden(s, c, k):
                for j in range(J):
                    act.wait_ge(sem("c0W", s), c["v"][j])
                    nc.scalar.activation(Z[s][:, j, :], Z[s][:, j, :], ACT.Relu).then_inc(sem("hidden_relu", s), 1)

            def hidden_scale(s, c, k):
                for j in range(J):
                    act.wait_ge(sem("lnz_ready", s), c["v"][j])
                    nc.scalar.activation(Z[s][:, j, :], Z[s][:, j, :], ACT.Identity, bias=NB[s][:, j:j + 1],
                                         scale=LN[s][:, RSTD, j:j + 1]).then_inc(sem("z_ready", s), 1)

            def relu(step):
                def f(s, c, k):
                    for j in range(J):
                        act.wait_ge(sem(f"p{step}", s), c["v"][j])
                        nc.scalar.activation(H[s][:, j, :], bank(s, step, j)[:, 0:D], ACT.Relu)\
                            .then_inc(sem(f"c{step}", s), 1)
                return f

            parts = {"P": prep, "B": by_members, "XB": shift, "P2": node_degrees, "P3": row_sums, "0W": hidden, "0Z": hidden_scale,
                     "G": take("G", G, P), "0U": take("0U", UHI, D), "1U": take("1U", UHI, DH),
                     "2U": take("2U", UHI, D), "3U": take("3U", UHI, D), "4U": take("4U", UHI, D), "5U": take("5U", UHI, D),
                     "6U": take("6U", UHI, D), "1W": lambda s, c, k: normalise(s, c, RES, "ln1_ready", "h1_ready"),
                     "2W": gcn, "2X": lambda s, c, k: normalise(s, c, RES, "ln2_ready", "h2_ready"),
                     "3S": scores, "3E": exps, "3W": lambda s, c, k: normalise(s, c, RES, "ln3_ready", "h3_ready"),
                     "4W": relu("4W"), "5W": relu("5W")}
            run(act, ACT_ORDER, parts)

        @block.vector
        def _(dve):
            dve.wait_ge(sem("setup_loaded"), 9 * 16)
            dve.wait_ge(sem("ones_ready"), 1)
            for m in range(HC):
                nc.vector.tensor_scalar(SPREAD[:, m, :], ONES[:, :], BETA[:, m:m + 1], None, ALU.mult)
                nc.vector.tensor_scalar(W2G[:, m, :], W2[:, m, :], GAMMA[:, m:m + 1], None, ALU.mult)\
                    .then_inc(sem("w2g_parts"), 1)
            for m in range(DC):
                last = nc.vector.tensor_scalar(SPREAD[:, HC + m, :], ONES[:, :], ACOL[:, m:m + 1], None, ALU.mult)
            last.then_inc(sem("spread_ready"), 1)
            dve.wait_ge(sem("w2g_parts"), HC)
            dve.wait_ge(sem("bw_product"), 1)
            nc.vector.tensor_copy(BW[:, :], WB[0][0][:, 0:D]).then_inc(sem("w2g_ready"), 1)
            dve.wait_ge(sem("wa_product"), 1)
            nc.vector.tensor_copy(WA[:, :], UB[0][0][:, 0:D]).then_inc(sem("bwwa_ready"), 1)
            dve.wait_ge(sem("bwwa_ready"), 1)
            dve.wait_ge(sem("w2g_ready"), 1)
            for step in W_STEPS:
                nc.vector.tensor_copy(WHI[step][:, :, :], RAW[step]).then_inc(sem("weights_high"), 1)
            dve.wait_ge(sem("weights_high"), len(W_STEPS))
            for step in W_STEPS:
                last = nc.vector.tensor_tensor(WLO[step][:, :, :], RAW[step], WHI[step][:, :, :].bitcast(F32),
                                               ALU.subtract)
            dve.wait_ge(sem("bias_loaded"), 96)
            for step, row in (("4W", L3B1), ("5W", L3B2)):
                nc.vector.tensor_copy(BIAS[step][:, :], row[0:2 * HALF, :]).then_inc(sem("bias_high"), 1)
            nc.vector.tensor_scalar(SHARES[:, :], ONES[0:2 * HALF, :], 1 / HALF, None, ALU.mult)
            dve.wait_ge(sem("bias_high"), 2)
            for step, row in (("4W", L3B1), ("5W", L3B2)):
                lower = BIAS[step][HALF:2 * HALF, :]
                last = nc.vector.tensor_tensor(lower, row[HALF:2 * HALF, :], lower.bitcast(F32), ALU.subtract)
            last.then_inc(sem("weights_split"), 1)
            dve.wait_ge(sem("weights_split"), 1)
            dve.wait_ge(sem("ident_ready"), 1)

            def stats(s, c, src, tag, waits):
                for j in range(J):
                    if waits:
                        dve.wait_ge(sem(waits), c["v"][j])
                    nc.vector.bn_stats(BN[s][:, j, :], src(j)).then_inc(sem("bn_stats" + tag), 1)
                dve.wait_ge(sem("bn_stats" + tag), c["v"][J - 1])
                nc.vector.tensor_tensor(LN[s][:, SUM, :], BN[s][:, :, 1], BN[s][:, :, 4], ALU.add)
                for j in range(J):
                    nc.vector.bn_aggr(MV[s][:, j, :], BN[s][:, j, :]).then_inc(sem("mv_ready" + tag), 1)

            def prep(s, c, k):
                dve.wait_ge(sem("x_loaded", s), c["dma"])
                stats(s, c, lambda j: X[s][:, j, :], "0", None)

            def degrees(s, c, k):
                v4 = c["v"][J - 1]
                row = lambda i: ST[s][:, i, :]
                dve.wait_ge(sem("t_loaded", s), c["dma"])
                for j in range(J):
                    nc.vector.tensor_scalar(HT[s][:, j, :], T[s][:, j, :], 0.0, 0.0, ALU.not_equal, ALU.add,
                                            accum_out=ST[s][:, CNT, j:j + 1]).then_inc(sem("ht_ready"), 1)
                dve.wait_ge(sem("r_loaded", s), c["dma"])
                dve.wait_ge(sem("w_loaded", s), c["dma"])
                for j in range(J):
                    nc.vector.scalar_tensor_tensor(JUNK[s][:, j, 1, :], R[s][:, j, :], 0.0, WR[s][:, j, :],
                                                   ALU.not_equal, ALU.mult, accum_out=ST[s][:, DNS, j:j + 1])\
                        .then_inc(sem("dns"), 1)
                dve.wait_ge(sem("ht_ready"), v4)
                nc.vector.tensor_scalar(row(CNM), row(CNT), 1.0, None, ALU.max).then_inc(sem("cnm"), J)
                dve.wait_ge(sem("dns"), v4)
                nc.vector.tensor_scalar(row(DN), row(DNS), TINY, None, ALU.max).then_inc(sem("dnm"), J)
                nc.vector.scalar_tensor_tensor(JUNK[s][:, 0, 0, :], R[s][:, 0, :], 0.0, IDENT[:, :],
                                               ALU.not_equal, ALU.max, accum_out=ST[s][:, DG1, 0:1])\
                    .then_inc(sem("deg_ready"), 1)
                dve.wait_ge(sem("cnm"), v4)
                nc.vector.reciprocal(row(BE), row(CNM)).then_inc(sem("be"), J)
                dve.wait_ge(sem("dnm"), v4)
                nc.vector.reciprocal(row(DNI), row(DN)).then_inc(sem("dni"), J)
                for j in range(1, J):
                    nc.vector.scalar_tensor_tensor(JUNK[s][:, j, 0, :], R[s][:, j, :], 0.0, IDENT[:, :],
                                                   ALU.not_equal, ALU.max, accum_out=ST[s][:, DG1, j:j + 1])\
                        .then_inc(sem("deg_ready"), 1)
                dve.wait_ge(sem("dni"), v4)
                nc.vector.scalar_tensor_tensor(row(DN), row(DNS), 0.0, row(DNI), ALU.is_gt,
                                               ALU.mult).then_inc(sem("dn_ready"), J)

            def prep_rest(s, c, k):
                v4 = c["v"][J - 1]
                dve.wait_ge(sem("dgh_ready"), v4)
                dve.wait_ge(sem("dn_ready"), v4)
                nc.vector.tensor_tensor(ST[s][:, S2, :], ST[s][:, DN, :], ST[s][:, DGH, :], ALU.mult)\
                    .then_inc(sem("s2"), J)

            def low(step, n):
                def f(s, c, k):
                    for j in range(J):
                        dve.wait_ge(sem(f"c{step}"), c["v"][j])
                        nc.vector.tensor_tensor(ULO[s][:, j, 0:n], bank(s, step, j)[:, 0:n],
                                                UHI[s][:, j, 0:n].bitcast(F32), ALU.subtract)\
                            .then_inc(sem(f"l{step}"), 1)
                return f

            def hidden(s, c, k):
                for j in range(J):
                    dve.wait_ge(sem("p0W", s), c["v"][j])
                    nc.vector.scalar_tensor_tensor(Z[s][:, j, :], bank(s, "0W", j)[:, 0:DH], ST[s][:, DN, j:j + 1], B1[:, :],
                                                   ALU.mult, ALU.add).then_inc(sem("c0W", s), 1)

            def hidden_norm(s, c, k):
                stats(s, c, lambda j: Z[s][:, j, :], "z", "hidden_relu")

            def conv_out(s, c, k):
                for j in range(J):
                    dve.wait_ge(sem("p1W", s), c["v"][j])
                    dve.wait_ge(sem("rest_ready", s), c["v"][j])
                    nc.vector.scalar_tensor_tensor(RES[s][:, j, :], bank(s, "1W", j)[:, 0:D], ST[s][:, DN, j:j + 1],
                                                   RES[s][:, j, :], ALU.mult, ALU.add).then_inc(sem("c1W", s), 1)

            def conv_stats(s, c, k):
                stats(s, c, lambda j: RES[s][:, j, :], "1", "c1W")

            def gcn_out(s, c, k):
                for j in range(J):
                    dve.wait_ge(sem("p2W", s), c["v"][j])
                    nc.vector.scalar_tensor_tensor(TMP[s][:, j, :], bank(s, "2W", j)[:, 0:D], ST[s][:, DINV, j:j + 1], L1B[:, :],
                                                   ALU.mult, ALU.add).then_inc(sem("c2W", s), 1)

            def gcn_stats(s, c, k):
                stats(s, c, lambda j: RES[s][:, j, :], "2", "x2_ready")

            def node_scores(s, c, k):
                for j in range(J):
                    dve.wait_ge(sem("h2_ready", s), c["v"][j])
                    nc.vector.scalar_tensor_tensor(Z[s][:, j, 0:D], H[s][:, j, :], 1.0, WA[:, :], ALU.mult, ALU.mult,
                                                   accum_out=ST[s][:, SC, j:j + 1]).then_inc(sem("s_ready", s), 1)

            def score_diagonal(s, c, k):
                for j in range(J):
                    dve.wait_ge(sem("s_ready", s), c["v"][j])
                    nc.vector.tensor_scalar(TMP[s][:, j, 0:P], IDENT[:, :], ST[s][:, SC, j:j + 1], None, ALU.mult)\
                        .then_inc(sem("diag_ready", s), 1)

            def scores(s, c, k):
                for j in range(J):
                    dve.wait_ge(sem("c3S", s), c["v"][j])
                    nc.vector.scalar_tensor_tensor(E[s][:, j, :], E[s][:, j, :], 0.1, E[s][:, j, :], ALU.mult,
                                                   ALU.max).then_inc(sem("leak_ready", s), 1)

            def attend(s, c, k):
                for j in range(J):
                    dve.wait_ge(sem("e_ready", s), c["v"][j])
                    nc.vector.tensor_tensor(AE[s][:, j, :], E[s][:, j, :], T[s][:, j, :], ALU.mult)\
                        .then_inc(sem("ae_ready", s), 1)

            def attention_sums(s, c, k):
                for j in range(J):
                    dve.wait_ge(sem("e_ready", s), c["v"][j])
                    nc.vector.scalar_tensor_tensor(JUNK[s][:, j, 1, :], E[s][:, j, :], 1.0, R[s][:, j, :], ALU.mult,
                                                   ALU.mult, accum_out=ST[s][:, RSA, j:j + 1])\
                        .then_inc(sem("rsa", s), 1)

            def attention_scales(s, c, k):
                dve.wait_ge(sem("rsa", s), c["v"][J - 1])
                nc.vector.reciprocal(ST[s][:, RSA, :], ST[s][:, RSA, :]).then_inc(sem("rsa_inv", s), J)
                dve.wait_ge(sem("rsa_inv", s), c["v"][J - 1])
                dve.wait_ge(sem("rsr_ready", s), c["v"][J - 1])
                nc.vector.tensor_tensor(ST[s][:, RR, :], ST[s][:, RSA, :], ST[s][:, RSR, :], ALU.mult)\
                    .then_inc(sem("rr_ready", s), J)

            def attention_out(s, c, k):
                dve.wait_ge(sem("rr_ready", s), c["v"][J - 1])
                for j in range(J):
                    dve.wait_ge(sem("p3W", s), c["v"][j])
                    nc.vector.scalar_tensor_tensor(RES[s][:, j, :], bank(s, "3W", j)[:, 0:D], ST[s][:, RR, j:j + 1],
                                                   RES[s][:, j, :], ALU.mult, ALU.add).then_inc(sem("c3W", s), 1)

            def attention_stats(s, c, k):
                stats(s, c, lambda j: RES[s][:, j, :], "3", "c3W")

            def last_out(s, c, k):
                dve.wait_ge(sem("stored", s), c["dma"])
                for j in range(J):
                    dve.wait_ge(sem("p6W", s), c["v"][j])
                    dve.wait_ge(sem("x3b_ready", s), c["v"][j])
                    nc.vector.tensor_tensor(O[s][:, j, :], bank(s, "6W", j)[:, 0:D], RES[s][:, j, :], ALU.add)\
                        .then_inc(sem("c6W", s), 1)

            parts = {"P": prep, "PT": degrees, "P2": prep_rest, "0W": hidden, "0N": hidden_norm, "1W": conv_out,
                     "1N": conv_stats, "2W": gcn_out, "2X": gcn_stats, "2S": node_scores, "2D": score_diagonal,
                     "3S": scores, "3E": attend, "3R": attention_sums, "3I": attention_scales, "3W": attention_out,
                     "3N": attention_stats, "6W": last_out,
                     **{f"{i}U": low(f"{i}U", DH if i == 1 else D) for i in range(7)}}
            run(dve, DVE_ORDER, parts)

        @block.gpsimd
        def _(pool):
            nc.gpsimd.memset(ONES[:, :], 1.0).then_inc(sem("ones_ready"), 1)
            nc.gpsimd.memset(EIGHTH[:, :], 0.125)
            nc.gpsimd.memset(EPS[:, :], LN_EPS)
            for s in STREAMS:
                nc.gpsimd.memset(NB[s][:, :], 0.0).then_inc(sem("stored", s), 16)
            nc.gpsimd.memset(MHALF[:, :], -0.5).then_inc(sem("mhalf_ready"), 1)
            nc.gpsimd.memset(IDENT[:, :], 0.0).then_inc(sem("zeros_ready"), 1)
            pool.wait_ge(sem("zeros_ready"), 1)
            nc.gpsimd.affine_select(out=IDENT[:, :], in_=IDENT[:, :], compare_op=ALU.not_equal, fill=1.0, base=0,
                                    pattern=[[-1, P]], channel_multiplier=1).then_inc(sem("ident_ready"), 1)
            pool.wait_ge(sem("ident_ready"), 1)
            nc.gpsimd.tensor_tensor(OFFDIAG[:, :], ONES[:, :], IDENT[:, :], ALU.subtract).then_inc(sem("offdiag_ready"), 1)
            pool.wait_ge(sem("mhalf_ready"), 1)
            pool.wait_ge(sem("offdiag_ready"), 1)
            pool.wait_ge(sem("bias_loaded"), 96)
            pool.wait_ge(sem("weights_split"), 1)

            def norm(s, c, tag, scale=None):
                v4, rstd = c["v"][J - 1], LN[s][:, RSTD, :]
                pool.wait_ge(sem("mv_ready" + tag), v4)
                nc.gpsimd.tensor_tensor(LN[s][:, VE, :], MV[s][:, :, 1], EPS[:, :], ALU.add).then_inc(sem("ve" + tag), J)
                nc.gpsimd.tensor_tensor(LN[s][:, NMU, :], LN[s][:, SUM, :], MHALF[:, :], ALU.mult)
                pool.wait_ge(sem("ve" + tag), v4)
                nc.gpsimd.tensor_tensor(rstd, LN[s][:, VE, :], MHALF[:, :], ALU.pow).then_inc(sem("rstd" + tag), J)
                pool.wait_ge(sem("rstd" + tag), v4)
                if scale is not None:
                    nc.gpsimd.tensor_tensor(rstd, rstd, scale, ALU.mult).then_inc(sem("rstd_scaled"), J)
                    pool.wait_ge(sem("rstd_scaled"), v4)
                nc.gpsimd.tensor_tensor(NB[s][:, :], LN[s][:, NMU, :], rstd, ALU.mult).then_inc(sem(f"ln{tag}_ready"), J)

            def prep(s, c, k):
                norm(s, c, "0")

            def with_loops(s, c, k):
                for j in range(J):
                    pool.wait_ge(sem("ht_ready", s), c["v"][j])
                    nc.gpsimd.tensor_tensor(AT[s][:, j, :], HT[s][:, j, :], OFFDIAG[:, :], ALU.mult)\
                        .then_inc(sem("at_offdiag", s), 1)
                for j in range(J):
                    pool.wait_ge(sem("at_offdiag", s), c["v"][j])
                    nc.gpsimd.tensor_tensor(AT[s][:, j, :], AT[s][:, j, :], IDENT[:, :], ALU.add)\
                        .then_inc(sem("at_ready", s), 1)

            def gcn_degrees(s, c, k):
                pool.wait_ge(sem("deg_ready", s), c["v"][J - 1])
                nc.gpsimd.tensor_tensor(ST[s][:, DINV, :], ST[s][:, DG1, :], MHALF[:, :], ALU.pow)\
                    .then_inc(sem("dinv", s), J)

            def rest(s, c, k):
                pool.wait_ge(sem("x_loaded", s), c["dma"])
                for j in range(J):
                    pool.wait_ge(sem("shift_ready"), c["v"][j])
                    nc.gpsimd.tensor_tensor(RES[s][:, j, :], TMP[s][:, j, :], X[s][:, j, :], ALU.add)\
                        .then_inc(sem("rest_x"), 1)
                for j in range(J):
                    pool.wait_ge(sem("rest_x"), c["v"][j])
                    nc.gpsimd.tensor_tensor(RES[s][:, j, :], RES[s][:, j, :], B2[:, :], ALU.add)\
                        .then_inc(sem("rest_b2", s), 1)
                for j in range(J):
                    pool.wait_ge(sem("rest_b2", s), c["v"][j])
                    pool.wait_ge(sem("h0_ready", s), c["v"][j])
                    nc.gpsimd.tensor_tensor(RES[s][:, j, :], RES[s][:, j, :], H[s][:, j, :], ALU.add)\
                        .then_inc(sem("rest_ready", s), 1)

            def conv(s, c, k):
                pool.wait_ge(sem("dinv", s), c["v"][J - 1])
                norm(s, c, "1", ST[s][:, DINV, :])

            def gcn_add(s, c, k):
                for j in range(J):
                    pool.wait_ge(sem("tanh_ready", s), c["v"][j])
                    nc.gpsimd.tensor_tensor(RES[s][:, j, :], RES[s][:, j, :], TMP[s][:, j, :], ALU.add)\
                        .then_inc(sem("x2_ready", s), 1)

            def gcn(s, c, k):
                norm(s, c, "2")

            def node_scores(s, c, k):
                pool.wait_ge(sem("s_ready", s), c["v"][J - 1])
                nc.gpsimd.tensor_tensor(ST[s][:, S8, :], ST[s][:, SC, :], EIGHTH[:, :], ALU.mult)\
                    .then_inc(sem("s8_ready", s), J)

            def attention(s, c, k):
                norm(s, c, "3")

            def last_bias(s, c, k):
                for j in range(J):
                    pool.wait_ge(sem("h3_ready", s), c["v"][j])
                    nc.gpsimd.tensor_tensor(RES[s][:, j, :], RES[s][:, j, :], L3B3[:, :], ALU.add)\
                        .then_inc(sem("x3b_ready", s), 1)

            parts = {"P": prep, "AT": with_loops, "DI": gcn_degrees, "R": rest, "0N": lambda s, c, k: norm(s, c, "z"), "1W": conv,
                     "2A": gcn_add, "2X": gcn, "2S": node_scores, "3W": attention, "X3": last_bias}
            run(pool, POOL_ORDER, parts)


def kernel(x, adj, L0_gnn_W1, L0_gnn_b1, L0_gnn_gamma, L0_gnn_beta, L0_gnn_W2, L0_gnn_b2, L1_gnn_W, L1_gnn_b,
           L2_gnn_w, L2_gnn_a, L3_gnn_W1, L3_gnn_b1, L3_gnn_W2, L3_gnn_b2, L3_gnn_W3, L3_gnn_b3):
    import numpy as np
    import concourse.bacc as bacc
    from concourse.bass_utils import run_bass_kernel_spmd as launch

    x, adj = np.asarray(x), np.asarray(adj)
    n, c, d = x.shape
    g = n // (len(STREAMS) * J)

    def grouped(a):
        return a.reshape(g, len(STREAMS), J, a.shape[1], a.shape[2]).transpose(0, 1, 3, 2, 4)

    def chunked(w):
        w = np.asarray(w)
        return w.reshape(-1, P, w.shape[1]).transpose(1, 0, 2)

    def column(v):
        return np.asarray(v).reshape(-1, P).T

    arrays = {
        "xs": grouped(x), "adj_t": grouped(adj.transpose(0, 2, 1)), "adj_r": grouped(adj),
        "adj_w": adj[:, 0, :].reshape(g, len(STREAMS), J, c),
        "w1t": chunked(np.asarray(L0_gnn_W1).T), "w2t": chunked(np.asarray(L0_gnn_W2).T), "l1w": chunked(L1_gnn_W),
        "l2w": chunked(L2_gnn_w), "l2wt": chunked(np.asarray(L2_gnn_w).T), "l3w1": chunked(L3_gnn_W1),
        "l3w2": chunked(L3_gnn_W2), "l3w3": chunked(L3_gnn_W3),
        "cols": np.concatenate([column(L0_gnn_gamma), column(L0_gnn_beta), column(L2_gnn_a)], axis=1),
        "b1": L0_gnn_b1, "b2": L0_gnn_b2, "l1b": L1_gnn_b, "l3b1": L3_gnn_b1, "l3b2": L3_gnn_b2, "l3b3": L3_gnn_b3}
    arrays = {k: np.ascontiguousarray(np.asarray(a)) for k, a in arrays.items()}
    nc = bacc.Bacc("TRN2", target_bir_lowering=False, num_devices=1)
    args = {k: nc.dram_tensor(f"in_{k}", a.shape, mybir.dt.from_np(a.dtype), kind="ExternalInput").ap()
            for k, a in arrays.items()}
    out = nc.dram_tensor("out_rows", arrays["xs"].shape, F32, kind="ExternalOutput").ap()
    program(nc, **args, out=out)
    r = launch(nc, [{f"in_{k}": a for k, a in arrays.items()}], core_ids=[0])
    rows = r.results[0]["out_rows"]
    return rows.transpose(0, 1, 3, 2, 4).reshape(n, c, d)
```

```python
from contextlib import ExitStack

import concourse.bass as bass
from concourse import mybir
from concourse.alu_op_type import AluOpType as ALU

F32 = mybir.dt.float32
F32R = mybir.dt.float32r
ACT = mybir.ActivationFunctionType
P = 128
J = 2
STREAMS = ("A", "B", "C", "D")
LN_EPS = 1e-5
HALF = 32
TINY = 1.1754944e-38

PE_SLOTS = {
    "G": 2.890, "0U": 3.256, "0W": 3.665, "1U": 4.986, "1W": 5.422, "2U": 7.425, "2W": 7.801, "3S": 9.193,
    "3U": 9.672, "3W": 10.446, "4U": 11.122, "4W": 11.483, "5U": 12.384, "5W": 12.888, "6U": 13.845, "6W": 14.116}
ACT_SLOTS = {
    "P": 0.386, "P3": 4.647, "B": 0.477, "XB": 1.929, "G": 0.842, "0U": 1.517, "0W": 2.308, "0Z": 2.531, "1U": 2.819,
    "1W": 5.069, "2U": 5.389, "2W": 5.755, "2X": 6.430, "2D": 6.685, "3S": 7.422, "3E": 7.522, "3U": 8.254,
    "3W": 8.901, "4U": 9.126, "4W": 9.780, "5U": 10.632, "5W": 11.502, "6U": 11.534}
DVE_SLOTS = {
    "P": 1.30, "PT": 1.77, "P2": 3.19, "0U": 3.11, "0W": 3.54, "0N": 3.81, "1U": 4.34, "1W": 5.44, "1N": 5.73,
    "2U": 6.85, "2W": 7.11, "2X": 7.70, "2S": 8.04, "2D": 8.62, "3S": 9.08, "3E": 9.21, "3R": 9.35, "3I": 9.67,
    "3U": 9.76, "3W": 10.00, "3N": 10.05, "4U": 11.03, "5U": 12.26, "6U": 13.32, "6W": 13.81}
POOL_SLOTS = {
    "P": 2.7, "AT": 6.2, "DI": 3.3, "R": 4.6, "0N": 5.2, "1W": 7.1, "2A": 8.4, "2X": 8.9, "2S": 9.5, "3W": 11.3,
    "X3": 12.8}
SP_SLOTS = {
    "X": -0.8, "T": 0.8, "O": 13.2}
SLOTS = 12


def ordered(slots):
    entries = []
    for i, s in enumerate(STREAMS):
        for step, at in slots.items():
            at += i * SLOTS / len(STREAMS)
            entries.append((at % SLOTS, s, step, -int(at // SLOTS)))
    return [x[1:] for x in sorted(entries)]


PE_ORDER, ACT_ORDER, DVE_ORDER, POOL_ORDER, SP_ORDER = map(ordered, (PE_SLOTS, ACT_SLOTS, DVE_SLOTS, POOL_SLOTS, SP_SLOTS))


def program(nc, xs, adj_t, adj_r, w1t, w2t, l1w, l2w, l2wt, l3w1, l3w2, l3w3,
            cols, b1, b2, l1b, l3b1, l3b2, l3b3, out):
    GROUPS = xs.shape[0]
    D = l1w.shape[2]
    DC = D // P
    DH = w1t.shape[2]
    HC = DH // P

    with ExitStack() as ctx:
        def sb(name, shape, dt=F32):
            return ctx.enter_context(nc.sbuf_tensor(name, shape, dt))

        sems = {}
        PER_STREAM = ("x_loaded", "t_loaded", "r_loaded", "stored")

        def sem(name, s=""):
            key = f"{name}_{s}" if name in PER_STREAM else name
            if key not in sems:
                sems[key] = ctx.enter_context(nc.semaphore(key))
            return sems[key]

        WIDTH = {"0W": (DC, DH), "1W": (HC, D), "2W": (DC, D), "3W": (DC, D), "4W": (DC, D), "5W": (DC, D), "6W": (DC, D)}
        WHI = {step: sb(f"WHI{step}", [P, *shape], F32R) for step, shape in WIDTH.items()}
        WLO = {step: sb(f"WLO{step}", [P, *shape], F32R) for step, shape in WIDTH.items()}
        COLS = sb("COLS", [P, 2 * HC + DC])
        GAMMA, BETA, ACOL = COLS[:, 0:HC], COLS[:, HC:2 * HC], COLS[:, 2 * HC:]
        B1 = sb("B1", [P, DH])
        B2, L1B, L3B1, L3B2, L3B3 = (sb(n, [P, D]) for n in ("B2", "L1B", "L3B1", "L3B2", "L3B3"))
        BIAS = {step: sb(f"BIAS{step}", [2 * HALF, D], F32R) for step in ("4W", "5W")}
        SHARES = sb("SHARES", [2 * HALF, P], F32R)
        BW = sb("BW", [P, D])
        WA = sb("WA", [P, D])
        SPREAD = sb("SPREAD", [P, HC + DC, P])
        IDENT = sb("IDENT", [P, P])
        ONES = sb("ONES", [P, P])
        OFFDIAG = sb("OFFDIAG", [P, P])
        ONESR = sb("ONESR", [P, P], F32R)
        JUNK = sb("JUNK", [P, J, 3, P])
        MHALF = sb("MHALF", [P, J])
        EIGHTH = sb("EIGHTH", [P, J])
        EPS = sb("EPS", [P, J])

        def per_stream(name, *shape):
            return {s: sb(f"{name}_{s}", [P, *shape]) for s in STREAMS}

        X = per_stream("X", J, D)
        T = per_stream("T", J, P)
        R = per_stream("R", J, P)
        HT = per_stream("HT", J, P)
        BHT = per_stream("BHT", J, P + 2)
        AT = per_stream("AT", J, P)
        G = per_stream("G", J, P + 2)
        H = per_stream("H", J, D)
        UHI = {s: sb(f"UHI_{s}", [P, J, DH], F32R) for s in STREAMS}
        ULO = {s: sb(f"ULO_{s}", [P, J, DH], F32R) for s in STREAMS}
        Z = per_stream("Z", J, DH)
        RES = per_stream("RES", J, D)
        TMP = per_stream("TMP", J, D)
        E = per_stream("E", J, P)
        AE = per_stream("AE", J, P)
        O = per_stream("O", J, D)
        BN = per_stream("BN", J, 6)
        MV = per_stream("MV", J, 2)
        LN = per_stream("LN", 4, J)
        SUM, VE, NMU, RSTD = range(4)
        NB = per_stream("NB", J)
        ST = per_stream("ST", 13, J)
        CNT, BE, DN, DNI, DG1, DINV, S2, RSR, RSA, RR, SC, S8, CNM = range(13)
        DNS, DGH = ({s: G[s][:, :, P + i] for s in STREAMS} for i in range(2))

        TURNS = 2
        UB = [[ctx.enter_context(nc.psum_tensor(f"UB{n}{j}", [P, 512], F32)) for j in range(J)] for n in range(TURNS)]
        WB = [[ctx.enter_context(nc.psum_tensor(f"WB{n}{j}", [P, 512], F32)) for j in range(J)] for n in range(TURNS)]
        U_STEPS = ("G", "3S") + tuple(f"{i}U" for i in range(7))
        W_STEPS = tuple(f"{i}W" for i in range(7))

        SETUP_BANKS = WB[1 - [x[:2] for x in PE_ORDER if x[1] in W_STEPS].index(("A", "0W")) % TURNS]

        def bank(s, step, j):
            kind, banks = (U_STEPS, UB) if step in U_STEPS else (W_STEPS, WB)
            return banks[[x[:2] for x in PE_ORDER if x[1] in kind].index((s, step)) % TURNS][j]

        W1, W2, W2G = sb("W1", [P, DC, DH]), sb("W2", [P, HC, D]), sb("W2G", [P, HC, D])
        L2WT = TMP["D"]
        RAW = {"0W": W1, "1W": W2G, "2W": O["A"], "3W": O["B"], "4W": O["C"], "5W": O["D"], "6W": RES["D"]}

        block = ctx.enter_context(nc.Block())

        def done_at(s, k, j):
            return len(STREAMS) * J * k + J * STREAMS.index(s) + j + 1

        LIVE = [(s, back) for s in STREAMS for back in (0, -1)]

        def run(eng, order, parts, setup={}):
            def values(k):
                return {(s, back): dict(v=[done_at(s, k + back, j) for j in range(J)], dma=16 * (k + back + 1))
                        for s, back in LIVE}

            for s, step, back in order:
                if not back:
                    parts[step](s, values(0)[s, 0], 0)
                    if (s, step) in setup:
                        setup[s, step]()
            with eng.Fori(1, GROUPS) as k:
                loop = {(s, back): dict(v=[eng.snap(len(STREAMS) * J * k + done_at(s, back, j)) for j in range(J)])
                        for s, back in LIVE}
                dma = {back: eng.snap(16 * k + 16 * (back + 1)) for back in (0, -1)}
                for s, back in LIVE:
                    loop[s, back]["dma"] = dma[back]
                for s, step, back in order:
                    parts[step](s, loop[s, back], loop)
            for s, step, back in order:
                if back:
                    parts[step](s, values(GROUPS)[s, back], GROUPS)

        @block.sync
        def _(sp):
            def load_x(s, group, n):
                if n is not None:
                    sp.wait_ge(sem("rest_ready"), n)
                sp.dma_start(X[s][:, :, :], xs[group, STREAMS.index(s)]).then_inc(sem("x_loaded", s), 16)

            def load_adj(s, group, n):
                i = STREAMS.index(s)
                if n is not None:
                    sp.wait_ge(sem("p6U"), n)
                sp.dma_start(T[s][:, :, :], adj_t[group, i]).then_inc(sem("t_loaded", s), 16)
                sp.dma_start(R[s][:, :, :], adj_r[group, i]).then_inc(sem("r_loaded", s), 16)

            def load(s, group, n):
                load_x(s, group, n)
                load_adj(s, group, n)

            def store(s, group, n):
                sp.wait_ge(sem("c6W"), n)
                sp.dma_start(out[group, STREAMS.index(s)], O[s][:, :, :]).then_inc(sem("stored", s), 16)

            load("A", 0, None)
            sp.dma_start(W1[:, :, :], w1t).then_inc(sem("w1_loaded"), 16)
            sp.dma_start(COLS[:, :], cols).then_inc(sem("cols_loaded"), 16)
            sp.dma_start(W2[:, :, :], w2t).then_inc(sem("w2_loaded"), 16)
            sp.dma_start(L2WT[:, :, :], l2wt).then_inc(sem("w2_loaded"), 16)
            for dst, src in ((B1, b1), (B2, b2), (L1B, l1b), (L3B1, l3b1), (L3B2, l3b2), (L3B3, l3b3)):
                sp.dma_start(dst[:, :], src.partition_broadcast(P)).then_inc(sem("bias_loaded"), 16)
            load("B", 0, None)
            for step, src in (("2W", l1w), ("3W", l2w), ("4W", l3w1), ("5W", l3w2), ("6W", l3w3)):
                sp.dma_start(RAW[step][:, :, :], src).then_inc(sem("weights_loaded"), 16)
            for s in STREAMS[2:]:
                load(s, 0, None)

            parts = {"X": load_x, "T": load_adj, "O": store}

            def one_pass(k):
                for s, step, back in SP_ORDER:
                    if isinstance(k, int) and not (0 if step == "O" else 1) <= k + back < GROUPS:
                        continue
                    before = back if step == "O" else back - 1
                    n = len(STREAMS) * J * k + done_at(s, before, J - 1)
                    parts[step](s, k + back, n if isinstance(k, int) else sp.snap(n))

            one_pass(0)
            with sp.Fori(1, GROUPS - 1) as k:
                one_pass(k)
            one_pass(GROUPS - 1)
            one_pass(GROUPS)
            for s in STREAMS:
                sp.wait_ge(sem("stored", s), 16 * (GROUPS + 1))

        @block.tensor
        def _(pe):
            def shifts():
                pe.wait_ge(sem("spread_ready"), 1)
                pe.wait_ge(sem("w2_loaded"), 32)
                for m in range(HC):
                    last = nc.tensor.matmul(SETUP_BANKS[0][:, 0:D], SPREAD[:, m, :], W2[:, m, :], start=(m == 0),
                                            stop=(m == HC - 1))
                for m in range(DC):
                    last = nc.tensor.matmul(SETUP_BANKS[1][:, 0:D], SPREAD[:, HC + m, :], L2WT[:, m, :], start=(m == 0),
                                            stop=(m == DC - 1))
                last.then_inc(sem("shift_products"), 1)

            def bank_free(s, step, c, k, j, kind):
                steps = [x for x in PE_ORDER if x[1] in kind]
                n = [x[:2] for x in steps].index((s, step))
                same = [(steps[m], 0) for m in range(n - TURNS, -1, -TURNS)]
                same += [(steps[m], 1) for m in range(len(steps) - 1, -1, -1) if (n - m) % TURNS == 0]
                for (s0, step0, back0), before in same:
                    if isinstance(k, dict):
                        value = k[s0, back0 - before]["v"][j]
                    else:
                        group = k - before + back0
                        if not 0 <= group < GROUPS:
                            continue
                        value = done_at(s0, group, j)
                    pe.wait_ge(sem(f"l{step0}" if step0[1:] == "U" else f"c{step0}"), value)
                    return

            def unit(step, lhs, rhs, chunks):
                def f(s, c, k):
                    for j in range(J):
                        if step in U_WAITS:
                            pe.wait_ge(sem(U_WAITS[step], s), c["v"][j])
                        if step in U_WAITS2:
                            pe.wait_ge(sem(U_WAITS2[step], s), c["v"][j])
                        bank_free(s, step, c, k, j, U_STEPS)
                        for m in range(chunks):
                            last = nc.tensor.matmul(bank(s, step, j)[:, m * P:(m + 1) * P], lhs(s, j)[:, m * P:(m + 1) * P],
                                                    rhs(s, j), start=True, stop=True)
                        last.then_inc(sem(f"p{step}"), 1)
                return f

            def weigh(step):
                chunks, n = WIDTH[step]
                hi, lo = WHI[step], WLO[step]

                def f(s, c, k):
                    for j in range(J):
                        if k == 0:
                            pe.wait_ge(sem("weights_split"), W_STEPS.index(step) + 1)
                        pe.wait_ge(sem(f"l{step[0]}U"), c["v"][j])
                        bank_free(s, step, c, k, j, W_STEPS)
                        terms = [(u[s][:, j, m * P:(m + 1) * P], w[:, m, :]) for m in range(chunks)
                                 for u, w in ((ULO, hi), (UHI, lo), (UHI, hi))]
                        if step in BIAS:
                            terms.insert(0, (SHARES[:, :], BIAS[step][:, :]))
                        for i, (u, w) in enumerate(terms):
                            last = nc.tensor.matmul(bank(s, step, j)[:, 0:n], u, w, start=(i == 0),
                                                    stop=(i == len(terms) - 1))
                        last.then_inc(sem(f"p{step}"), 1)
                return f

            def g_and_sums(s, c, k):
                for j in range(J):
                    pe.wait_ge(sem("weights_placed"), c["v"][j])
                    pe.wait_ge(sem("bht_ready"), c["v"][j])
                    bank_free(s, "G", c, k, j, U_STEPS)
                    nc.tensor.matmul(bank(s, "G", j)[:, 0:P + 2], HT[s][:, j, :], BHT[s][:, j, :], start=True,
                                     stop=True).then_inc(sem("pG"), 1)

            def spread_scores(s, c, k):
                pe.wait_ge(sem("diag_ready"), c["v"][J - 1])
                bank_free(s, "3S", c, k, J - 1, U_STEPS)
                for diag in (UHI, ULO):
                    last = nc.tensor.matmul(bank(s, "3S", J - 1)[:, 0:J * P], ONESR[:, :], diag[s][:, 0, 0:J * P],
                                            start=(diag is UHI), stop=(diag is ULO))
                last.then_inc(sem("p3S"), J)

            U_WAITS = {"0U": "h0_ready", "1U": "z_ready", "2U": "h1_ready", "3U": "ae_ready", "4U": "h3_ready",
                       "5U": "c4W", "6U": "c5W"}
            U_WAITS2 = {"0U": "cG", "2U": "at_ready"}
            parts = {
                "G": g_and_sums,
                "0U": unit("0U", lambda s, j: H[s][:, j, :], lambda s, j: G[s][:, j, 0:P], DC),
                "1U": unit("1U", lambda s, j: Z[s][:, j, :], lambda s, j: G[s][:, j, 0:P], HC),
                "2U": unit("2U", lambda s, j: H[s][:, j, :], lambda s, j: AT[s][:, j, :], DC),
                "3S": spread_scores,
                "3U": unit("3U", lambda s, j: H[s][:, j, :], lambda s, j: AE[s][:, j, :], DC),
                "4U": unit("4U", lambda s, j: H[s][:, j, :], lambda s, j: T[s][:, j, :], DC),
                "5U": unit("5U", lambda s, j: H[s][:, j, :], lambda s, j: T[s][:, j, :], DC),
                "6U": unit("6U", lambda s, j: H[s][:, j, :], lambda s, j: T[s][:, j, :], DC),
                **{step: weigh(step) for step in W_STEPS}}

            run(pe, PE_ORDER, parts, {("A", "0U"): shifts, ("A", "0W"): lambda: pe.wait_ge(sem("shifts_ready"), 1)})

        @block.scalar
        def _(act):
            def take(step, dst, n):
                def f(s, c, k):
                    for j in range(J):
                        act.wait_ge(sem(f"p{step}"), c["v"][j])
                        nc.scalar.activation(dst[s][:, j, 0:n], bank(s, step, j)[:, 0:n], ACT.Copy).then_inc(sem(f"c{step}"), 1)
                return f

            def normalise(s, c, src, waits, done):
                for j in range(J):
                    act.wait_ge(sem(waits), c["v"][j])
                    nc.scalar.activation(H[s][:, j, :], src[s][:, j, :], ACT.Relu, bias=NB[s][:, j:j + 1],
                                         scale=LN[s][:, RSTD, j:j + 1]).then_inc(sem(done), 1)

            def prep(s, c, k):
                normalise(s, c, X, "ln0_ready", "h0_ready")

            def by_members(s, c, k):
                for j in range(J):
                    act.wait_ge(sem("be"), c["v"][j])
                    nc.scalar.activation(BHT[s][:, j, 0:P], HT[s][:, j, :], ACT.Copy, scale=ST[s][:, BE, j:j + 1])\
                        .then_inc(sem("bht_ready"), 1)

            def shift(s, c, k):
                if k == 0:
                    act.wait_ge(sem("shifts_ready"), 1)
                for j in range(J):
                    act.wait_ge(sem("s2"), c["v"][j])
                    nc.scalar.activation(TMP[s][:, j, :], BW[:, :], ACT.Copy, scale=ST[s][:, S2, j:j + 1])\
                        .then_inc(sem("shift_ready"), 1)

            def row_sums(s, c, k):
                act.wait_ge(sem("r_loaded", s), c["dma"])
                for j in range(J):
                    nc.scalar.activation(JUNK[:, j, 2, :], R[s][:, j, :], ACT.Copy,
                                         accum_out=ST[s][:, RSR, j:j + 1]).then_inc(sem("rsr_ready"), 1)

            def gcn(s, c, k):
                for j in range(J):
                    act.wait_ge(sem("c2W"), c["v"][j])
                    nc.scalar.activation(TMP[s][:, j, :], TMP[s][:, j, :], ACT.Tanh).then_inc(sem("tanh_ready"), 1)

            def scores(s, c, k):
                for j in range(J):
                    act.wait_ge(sem("p3S"), c["v"][j])
                    act.wait_ge(sem("s8_ready"), c["v"][j])
                    nc.scalar.activation(E[s][:, j, :], bank(s, "3S", J - 1)[:, j * P:(j + 1) * P], ACT.Tanh, bias=ST[s][:, S8, j:j + 1],
                                         scale=0.125).then_inc(sem("c3S"), 1)

            def score_diagonal(s, c, k):
                for j in range(J):
                    act.wait_ge(sem("s_ready"), c["v"][j])
                    nc.scalar.activation(UHI[s][:, 0, j * P:(j + 1) * P], IDENT[:, :], ACT.Copy, scale=ST[s][:, SC, j:j + 1])\
                        .then_inc(sem("diag_high"), 1)

            def exps(s, c, k):
                for j in range(J):
                    act.wait_ge(sem("leak_ready"), c["v"][j])
                    nc.scalar.activation(E[s][:, j, :], E[s][:, j, :], ACT.Exp, scale=8.0).then_inc(sem("e_ready"), 1)

            def hidden(s, c, k):
                for j in range(J):
                    act.wait_ge(sem("c0W"), c["v"][j])
                    nc.scalar.activation(Z[s][:, j, :], Z[s][:, j, :], ACT.Relu).then_inc(sem("hidden_relu"), 1)

            def hidden_scale(s, c, k):
                for j in range(J):
                    act.wait_ge(sem("lnz_ready"), c["v"][j])
                    nc.scalar.activation(Z[s][:, j, :], Z[s][:, j, :], ACT.Identity, bias=NB[s][:, j:j + 1],
                                         scale=LN[s][:, RSTD, j:j + 1]).then_inc(sem("z_ready"), 1)

            def relu(step):
                def f(s, c, k):
                    for j in range(J):
                        act.wait_ge(sem(f"p{step}"), c["v"][j])
                        nc.scalar.activation(H[s][:, j, :], bank(s, step, j)[:, 0:D], ACT.Relu)\
                            .then_inc(sem(f"c{step}"), 1)
                return f

            parts = {"P": prep, "B": by_members, "XB": shift, "P3": row_sums, "0W": hidden, "0Z": hidden_scale,
                     "G": take("G", G, P + 2), "0U": take("0U", UHI, D), "1U": take("1U", UHI, DH),
                     "2U": take("2U", UHI, D), "3U": take("3U", UHI, D), "4U": take("4U", UHI, D), "5U": take("5U", UHI, D),
                     "6U": take("6U", UHI, D), "1W": lambda s, c, k: normalise(s, c, RES, "ln1_ready", "h1_ready"),
                     "2W": gcn, "2X": lambda s, c, k: normalise(s, c, RES, "ln2_ready", "h2_ready"),
                     "2D": score_diagonal, "3S": scores, "3E": exps, "3W": lambda s, c, k: normalise(s, c, RES, "ln3_ready", "h3_ready"),
                     "4W": relu("4W"), "5W": relu("5W")}
            def high(steps, waits, value):
                act.wait_ge(sem(waits), value)
                for step in steps:
                    nc.scalar.activation(WHI[step][:, :, :], RAW[step][:, :, :], ACT.Copy).then_inc(sem("weights_high"), 1)

            high(("0W",), "w1_loaded", 16)
            run(act, ACT_ORDER, parts, {("A", "0U"): lambda: high(("1W",), "w2g_ready", HC),
                                        ("A", "0W"): lambda: high(W_STEPS[2:], "weights_loaded", 5 * 16)})

        @block.vector
        def _(dve):
            def spread():
                dve.wait_ge(sem("cols_loaded"), 16)
                for m in range(HC):
                    nc.vector.tensor_scalar(SPREAD[:, m, :], ONES[:, :], BETA[:, m:m + 1], None, ALU.mult)
                for m in range(DC):
                    last = nc.vector.tensor_scalar(SPREAD[:, HC + m, :], ONES[:, :], ACOL[:, m:m + 1], None, ALU.mult)
                last.then_inc(sem("spread_ready"), 1)

            def low_weights(step):
                dve.wait_ge(sem("weights_high"), W_STEPS.index(step) + 1)
                nc.vector.tensor_tensor(WLO[step][:, :, :], RAW[step][:, :, :], WHI[step][:, :, :].bitcast(F32),
                                        ALU.subtract).then_inc(sem("weights_split"), 1)

            def first_weights():
                spread()
                low_weights("0W")

            def gamma_weights():
                dve.wait_ge(sem("w2_loaded"), 32)
                for m in range(HC):
                    nc.vector.tensor_scalar(W2G[:, m, :], W2[:, m, :], GAMMA[:, m:m + 1], None, ALU.mult)\
                        .then_inc(sem("w2g_ready"), 1)
                dve.wait_ge(sem("shift_products"), 1)
                nc.vector.tensor_copy(BW[:, :], SETUP_BANKS[0][:, 0:D])
                nc.vector.tensor_copy(WA[:, :], SETUP_BANKS[1][:, 0:D]).then_inc(sem("shifts_ready"), 1)
                nc.vector.tensor_copy(ONESR[:, :], ONES[:, :])

            def last_weights():
                low_weights("1W")
                nc.vector.tensor_scalar(SHARES[:, :], ONES[0:2 * HALF, :], 1 / HALF, None, ALU.mult)
                for step, row in (("4W", L3B1), ("5W", L3B2)):
                    nc.vector.tensor_copy(BIAS[step][:, :], row[0:2 * HALF, :]).then_inc(sem("bias_high"), 1)
                dve.wait_ge(sem("bias_high"), 2)
                for step, row in (("4W", L3B1), ("5W", L3B2)):
                    lower = BIAS[step][HALF:2 * HALF, :]
                    nc.vector.tensor_tensor(lower, row[HALF:2 * HALF, :], lower.bitcast(F32), ALU.subtract)
                for step in W_STEPS[2:]:
                    low_weights(step)

            dve.wait_ge(sem("ones_ready"), 1)

            def stats(s, c, src, tag, waits):
                for j in range(J):
                    if waits:
                        dve.wait_ge(sem(waits), c["v"][j])
                    nc.vector.bn_stats(BN[s][:, j, :], src(j)).then_inc(sem("bn_stats" + tag), 1)
                dve.wait_ge(sem("bn_stats" + tag), c["v"][J - 1])
                nc.vector.tensor_tensor(LN[s][:, SUM, :], BN[s][:, :, 1], BN[s][:, :, 4], ALU.add)
                for j in range(J):
                    nc.vector.bn_aggr(MV[s][:, j, :], BN[s][:, j, :]).then_inc(sem("mv_ready" + tag), 1)

            def prep(s, c, k):
                dve.wait_ge(sem("x_loaded", s), c["dma"])
                stats(s, c, lambda j: X[s][:, j, :], "0", None)

            def degrees(s, c, k):
                v = c["v"][J - 1]
                if k == 0:
                    dve.wait_ge(sem("ident_ready"), 1)
                dve.wait_ge(sem("t_loaded", s), c["dma"])
                for j in range(J):
                    nc.vector.tensor_scalar(HT[s][:, j, :], T[s][:, j, :], 0.0, 0.0, ALU.not_equal, ALU.add,
                                            accum_out=ST[s][:, CNT, j:j + 1]).then_inc(sem("ht_ready"), 1)
                nc.vector.tensor_copy(BHT[s][:, :, P], T[s][:, :, 0]).then_inc(sem("weights_placed"), J)
                dve.wait_ge(sem("ht_ready"), v)
                nc.vector.tensor_scalar(ST[s][:, CNM, :], ST[s][:, CNT, :], 1.0, None, ALU.max).then_inc(sem("cnm"), J)
                dve.wait_ge(sem("r_loaded", s), c["dma"])
                for j in range(J):
                    nc.vector.scalar_tensor_tensor(JUNK[:, j, 0, :], R[s][:, j, :], 0.0, IDENT[:, :],
                                                   ALU.not_equal, ALU.max, accum_out=ST[s][:, DG1, j:j + 1])\
                        .then_inc(sem("deg_ready"), 1)
                    if j == 0:
                        dve.wait_ge(sem("cnm"), v)
                        nc.vector.reciprocal(ST[s][:, BE, :], ST[s][:, CNM, :]).then_inc(sem("be"), J)

            def prep_rest(s, c, k):
                v = c["v"][J - 1]
                dve.wait_ge(sem("cG"), v)
                nc.vector.tensor_scalar(ST[s][:, DN, :], DNS[s], TINY, None, ALU.max).then_inc(sem("dnm"), J)
                dve.wait_ge(sem("dnm"), v)
                nc.vector.reciprocal(ST[s][:, DNI, :], ST[s][:, DN, :]).then_inc(sem("dni"), J)
                dve.wait_ge(sem("dni"), v)
                nc.vector.scalar_tensor_tensor(ST[s][:, DN, :], DNS[s], 0.0, ST[s][:, DNI, :], ALU.is_gt,
                                               ALU.mult).then_inc(sem("dn_ready"), J)
                dve.wait_ge(sem("dn_ready"), v)
                nc.vector.tensor_tensor(ST[s][:, S2, :], ST[s][:, DN, :], DGH[s], ALU.mult).then_inc(sem("s2"), J)

            def low(step, n):
                def f(s, c, k):
                    for j in range(J):
                        dve.wait_ge(sem(f"c{step}"), c["v"][j])
                        nc.vector.tensor_tensor(ULO[s][:, j, 0:n], bank(s, step, j)[:, 0:n],
                                                UHI[s][:, j, 0:n].bitcast(F32), ALU.subtract)\
                            .then_inc(sem(f"l{step}"), 1)
                return f

            def hidden(s, c, k):
                if k == 0:
                    dve.wait_ge(sem("bias_loaded"), 6 * 16)
                for j in range(J):
                    dve.wait_ge(sem("p0W"), c["v"][j])
                    nc.vector.scalar_tensor_tensor(Z[s][:, j, :], bank(s, "0W", j)[:, 0:DH], ST[s][:, DN, j:j + 1], B1[:, :],
                                                   ALU.mult, ALU.add).then_inc(sem("c0W"), 1)

            def hidden_norm(s, c, k):
                stats(s, c, lambda j: Z[s][:, j, :], "z", "hidden_relu")

            def conv_out(s, c, k):
                for j in range(J):
                    dve.wait_ge(sem("p1W"), c["v"][j])
                    dve.wait_ge(sem("rest_ready"), c["v"][j])
                    nc.vector.scalar_tensor_tensor(RES[s][:, j, :], bank(s, "1W", j)[:, 0:D], ST[s][:, DN, j:j + 1],
                                                   RES[s][:, j, :], ALU.mult, ALU.add).then_inc(sem("c1W"), 1)

            def conv_stats(s, c, k):
                stats(s, c, lambda j: RES[s][:, j, :], "1", "c1W")

            def gcn_out(s, c, k):
                for j in range(J):
                    dve.wait_ge(sem("p2W"), c["v"][j])
                    nc.vector.scalar_tensor_tensor(TMP[s][:, j, :], bank(s, "2W", j)[:, 0:D], ST[s][:, DINV, j:j + 1], L1B[:, :],
                                                   ALU.mult, ALU.add).then_inc(sem("c2W"), 1)

            def gcn_stats(s, c, k):
                stats(s, c, lambda j: RES[s][:, j, :], "2", "x2_ready")

            def node_scores(s, c, k):
                if k == 0:
                    dve.wait_ge(sem("shifts_ready"), 1)
                for j in range(J):
                    dve.wait_ge(sem("h2_ready"), c["v"][j])
                    nc.vector.scalar_tensor_tensor(Z[s][:, j, 0:D], H[s][:, j, :], 1.0, WA[:, :], ALU.mult, ALU.mult,
                                                   accum_out=ST[s][:, SC, j:j + 1]).then_inc(sem("s_ready"), 1)

            def score_diagonal(s, c, k):
                for j in range(J):
                    dve.wait_ge(sem("diag_high"), c["v"][j])
                    half = slice(j * P, (j + 1) * P)
                    nc.vector.scalar_tensor_tensor(ULO[s][:, 0, half], IDENT[:, :], ST[s][:, SC, j:j + 1],
                                                   UHI[s][:, 0, half].bitcast(F32), ALU.mult, ALU.subtract)\
                        .then_inc(sem("diag_ready"), 1)

            def scores(s, c, k):
                for j in range(J):
                    dve.wait_ge(sem("c3S"), c["v"][j])
                    nc.vector.scalar_tensor_tensor(E[s][:, j, :], E[s][:, j, :], 0.1, E[s][:, j, :], ALU.mult,
                                                   ALU.max).then_inc(sem("leak_ready"), 1)

            def attend(s, c, k):
                for j in range(J):
                    dve.wait_ge(sem("e_ready"), c["v"][j])
                    nc.vector.tensor_tensor(AE[s][:, j, :], E[s][:, j, :], T[s][:, j, :], ALU.mult)\
                        .then_inc(sem("ae_ready"), 1)

            def attention_sums(s, c, k):
                for j in range(J):
                    dve.wait_ge(sem("e_ready"), c["v"][j])
                    nc.vector.scalar_tensor_tensor(JUNK[:, j, 1, :], E[s][:, j, :], 1.0, R[s][:, j, :], ALU.mult,
                                                   ALU.mult, accum_out=ST[s][:, RSA, j:j + 1])\
                        .then_inc(sem("rsa"), 1)

            def attention_scales(s, c, k):
                dve.wait_ge(sem("rsa"), c["v"][J - 1])
                nc.vector.reciprocal(ST[s][:, RSA, :], ST[s][:, RSA, :]).then_inc(sem("rsa_inv"), J)
                dve.wait_ge(sem("rsa_inv"), c["v"][J - 1])
                dve.wait_ge(sem("rsr_ready"), c["v"][J - 1])
                nc.vector.tensor_tensor(ST[s][:, RR, :], ST[s][:, RSA, :], ST[s][:, RSR, :], ALU.mult)\
                    .then_inc(sem("rr_ready"), J)

            def attention_out(s, c, k):
                dve.wait_ge(sem("rr_ready"), c["v"][J - 1])
                for j in range(J):
                    dve.wait_ge(sem("p3W"), c["v"][j])
                    nc.vector.scalar_tensor_tensor(RES[s][:, j, :], bank(s, "3W", j)[:, 0:D], ST[s][:, RR, j:j + 1],
                                                   RES[s][:, j, :], ALU.mult, ALU.add).then_inc(sem("c3W"), 1)

            def attention_stats(s, c, k):
                stats(s, c, lambda j: RES[s][:, j, :], "3", "c3W")

            def last_out(s, c, k):
                dve.wait_ge(sem("stored", s), c["dma"])
                for j in range(J):
                    dve.wait_ge(sem("p6W"), c["v"][j])
                    dve.wait_ge(sem("x3b_ready"), c["v"][j])
                    nc.vector.tensor_tensor(O[s][:, j, :], bank(s, "6W", j)[:, 0:D], RES[s][:, j, :], ALU.add)\
                        .then_inc(sem("c6W"), 1)

            parts = {"P": prep, "PT": degrees, "P2": prep_rest, "0W": hidden, "0N": hidden_norm, "1W": conv_out,
                     "1N": conv_stats, "2W": gcn_out, "2X": gcn_stats, "2S": node_scores, "2D": score_diagonal,
                     "3S": scores, "3E": attend, "3R": attention_sums, "3I": attention_scales, "3W": attention_out,
                     "3N": attention_stats, "6W": last_out,
                     **{f"{i}U": low(f"{i}U", DH if i == 1 else D) for i in range(7)}}
            run(dve, DVE_ORDER, parts, {("A", "PT"): first_weights, ("A", "0U"): gamma_weights,
                                        ("A", "0N"): last_weights})

        @block.gpsimd
        def _(pool):
            for s in STREAMS:
                nc.gpsimd.memset(BHT[s][:, :, P + 1], 1.0)
            nc.gpsimd.memset(ONES[:, :], 1.0).then_inc(sem("ones_ready"), 1)
            nc.gpsimd.memset(EIGHTH[:, :], 0.125)
            nc.gpsimd.memset(EPS[:, :], LN_EPS)
            for s in STREAMS:
                nc.gpsimd.memset(NB[s][:, :], 0.0).then_inc(sem("stored", s), 16)
            nc.gpsimd.memset(MHALF[:, :], -0.5).then_inc(sem("mhalf_ready"), 1)
            nc.gpsimd.memset(IDENT[:, :], 0.0).then_inc(sem("zeros_ready"), 1)
            pool.wait_ge(sem("zeros_ready"), 1)
            nc.gpsimd.affine_select(out=IDENT[:, :], in_=IDENT[:, :], compare_op=ALU.not_equal, fill=1.0, base=0,
                                    pattern=[[-1, P]], channel_multiplier=1).then_inc(sem("ident_ready"), 1)
            pool.wait_ge(sem("ident_ready"), 1)
            nc.gpsimd.tensor_tensor(OFFDIAG[:, :], ONES[:, :], IDENT[:, :], ALU.subtract).then_inc(sem("offdiag_ready"), 1)
            pool.wait_ge(sem("mhalf_ready"), 1)
            pool.wait_ge(sem("offdiag_ready"), 1)

            def norm(s, c, tag, scale=None):
                v, rstd = c["v"][J - 1], LN[s][:, RSTD, :]
                pool.wait_ge(sem("mv_ready" + tag), v)
                nc.gpsimd.tensor_tensor(LN[s][:, VE, :], MV[s][:, :, 1], EPS[:, :], ALU.add).then_inc(sem("ve" + tag), J)
                nc.gpsimd.tensor_tensor(LN[s][:, NMU, :], LN[s][:, SUM, :], MHALF[:, :], ALU.mult)
                pool.wait_ge(sem("ve" + tag), v)
                nc.gpsimd.tensor_tensor(rstd, LN[s][:, VE, :], MHALF[:, :], ALU.pow).then_inc(sem("rstd" + tag), J)
                pool.wait_ge(sem("rstd" + tag), v)
                if scale is not None:
                    nc.gpsimd.tensor_tensor(rstd, rstd, scale, ALU.mult).then_inc(sem("rstd_scaled"), J)
                    pool.wait_ge(sem("rstd_scaled"), v)
                nc.gpsimd.tensor_tensor(NB[s][:, :], LN[s][:, NMU, :], rstd, ALU.mult).then_inc(sem(f"ln{tag}_ready"), J)

            def prep(s, c, k):
                norm(s, c, "0")

            def with_loops(s, c, k):
                for j in range(J):
                    pool.wait_ge(sem("ht_ready"), c["v"][j])
                    nc.gpsimd.tensor_tensor(AT[s][:, j, :], HT[s][:, j, :], OFFDIAG[:, :], ALU.mult)\
                        .then_inc(sem("at_offdiag"), 1)
                for j in range(J):
                    pool.wait_ge(sem("at_offdiag"), c["v"][j])
                    nc.gpsimd.tensor_tensor(AT[s][:, j, :], AT[s][:, j, :], IDENT[:, :], ALU.add)\
                        .then_inc(sem("at_ready"), 1)

            def gcn_degrees(s, c, k):
                pool.wait_ge(sem("deg_ready"), c["v"][J - 1])
                nc.gpsimd.tensor_tensor(ST[s][:, DINV, :], ST[s][:, DG1, :], MHALF[:, :], ALU.pow)\
                    .then_inc(sem("dinv"), J)

            def rest(s, c, k):
                if k == 0:
                    pool.wait_ge(sem("bias_loaded"), 6 * 16)
                pool.wait_ge(sem("x_loaded", s), c["dma"])
                for j in range(J):
                    pool.wait_ge(sem("shift_ready"), c["v"][j])
                    nc.gpsimd.tensor_tensor(RES[s][:, j, :], TMP[s][:, j, :], X[s][:, j, :], ALU.add)\
                        .then_inc(sem("rest_x"), 1)
                for j in range(J):
                    pool.wait_ge(sem("rest_x"), c["v"][j])
                    nc.gpsimd.tensor_tensor(RES[s][:, j, :], RES[s][:, j, :], B2[:, :], ALU.add)\
                        .then_inc(sem("rest_b2"), 1)
                for j in range(J):
                    pool.wait_ge(sem("rest_b2"), c["v"][j])
                    pool.wait_ge(sem("h0_ready"), c["v"][j])
                    nc.gpsimd.tensor_tensor(RES[s][:, j, :], RES[s][:, j, :], H[s][:, j, :], ALU.add)\
                        .then_inc(sem("rest_ready"), 1)

            def conv(s, c, k):
                pool.wait_ge(sem("dinv"), c["v"][J - 1])
                norm(s, c, "1", ST[s][:, DINV, :])

            def gcn_add(s, c, k):
                for j in range(J):
                    pool.wait_ge(sem("tanh_ready"), c["v"][j])
                    nc.gpsimd.tensor_tensor(RES[s][:, j, :], RES[s][:, j, :], TMP[s][:, j, :], ALU.add)\
                        .then_inc(sem("x2_ready"), 1)

            def gcn(s, c, k):
                norm(s, c, "2")

            def node_scores(s, c, k):
                pool.wait_ge(sem("s_ready"), c["v"][J - 1])
                nc.gpsimd.tensor_tensor(ST[s][:, S8, :], ST[s][:, SC, :], EIGHTH[:, :], ALU.mult)\
                    .then_inc(sem("s8_ready"), J)

            def attention(s, c, k):
                norm(s, c, "3")

            def last_bias(s, c, k):
                for j in range(J):
                    pool.wait_ge(sem("h3_ready"), c["v"][j])
                    nc.gpsimd.tensor_tensor(RES[s][:, j, :], RES[s][:, j, :], L3B3[:, :], ALU.add)\
                        .then_inc(sem("x3b_ready"), 1)

            parts = {"P": prep, "AT": with_loops, "DI": gcn_degrees, "R": rest, "0N": lambda s, c, k: norm(s, c, "z"), "1W": conv,
                     "2A": gcn_add, "2X": gcn, "2S": node_scores, "3W": attention, "X3": last_bias}
            run(pool, POOL_ORDER, parts)


def kernel(x, adj, L0_gnn_W1, L0_gnn_b1, L0_gnn_gamma, L0_gnn_beta, L0_gnn_W2, L0_gnn_b2, L1_gnn_W, L1_gnn_b,
           L2_gnn_w, L2_gnn_a, L3_gnn_W1, L3_gnn_b1, L3_gnn_W2, L3_gnn_b2, L3_gnn_W3, L3_gnn_b3):
    import numpy as np
    import concourse.bacc as bacc
    from concourse.bass_utils import run_bass_kernel_spmd as launch

    x, adj = np.asarray(x), np.asarray(adj)
    n, c, d = x.shape
    g = n // (len(STREAMS) * J)

    def grouped(a):
        return a.reshape(g, len(STREAMS), J, a.shape[1], a.shape[2]).transpose(0, 1, 3, 2, 4)

    def chunked(w):
        w = np.asarray(w)
        return w.reshape(-1, P, w.shape[1]).transpose(1, 0, 2)

    def column(v):
        return np.asarray(v).reshape(-1, P).T

    arrays = {
        "xs": grouped(x), "adj_t": grouped(adj.transpose(0, 2, 1)), "adj_r": grouped(adj),
        "w1t": chunked(np.asarray(L0_gnn_W1).T), "w2t": chunked(np.asarray(L0_gnn_W2).T), "l1w": chunked(L1_gnn_W),
        "l2w": chunked(L2_gnn_w), "l2wt": chunked(np.asarray(L2_gnn_w).T), "l3w1": chunked(L3_gnn_W1),
        "l3w2": chunked(L3_gnn_W2), "l3w3": chunked(L3_gnn_W3),
        "cols": np.concatenate([column(L0_gnn_gamma), column(L0_gnn_beta), column(L2_gnn_a)], axis=1),
        "b1": L0_gnn_b1, "b2": L0_gnn_b2, "l1b": L1_gnn_b, "l3b1": L3_gnn_b1, "l3b2": L3_gnn_b2, "l3b3": L3_gnn_b3}
    arrays = {k: np.ascontiguousarray(np.asarray(a)) for k, a in arrays.items()}
    nc = bacc.Bacc("TRN2", target_bir_lowering=False, num_devices=1)
    args = {k: nc.dram_tensor(f"in_{k}", a.shape, mybir.dt.from_np(a.dtype), kind="ExternalInput").ap()
            for k, a in arrays.items()}
    out = nc.dram_tensor("out_rows", arrays["xs"].shape, F32, kind="ExternalOutput").ap()
    program(nc, **args, out=out)
    r = launch(nc, [{f"in_{k}": a for k, a in arrays.items()}], core_ids=[0])
    rows = r.results[0]["out_rows"]
    return rows.transpose(0, 1, 3, 2, 4).reshape(n, c, d)
```
